# Optimizing a Trainium2 kernel written in Bass

```python
import numpy as np
import jax
import jax.numpy as jnp

def _softmax(x, axis=-1):
    return jax.nn.softmax(x, axis=axis)

def _gelu(x):
    return jax.nn.gelu(x, approximate=True)

def _silu(x):
    return jax.nn.silu(x)

def _sigmoid(x):
    return jax.nn.sigmoid(x)

def _layernorm(x, axis=-1, eps=1e-05):
    m = jnp.mean(x, axis=axis, keepdims=True)
    v = jnp.var(x, axis=axis, keepdims=True)
    return (x - m) / jnp.sqrt(v + eps)

def _scatter_add(tgt, idx, src, axis=0):
    return tgt.at[idx].add(src)

def _segment_sum(src, seg, n):
    return jax.ops.segment_sum(src, seg, n)
kernel_name = 'mk_prb_d1_jaxref_r8_040e68'

def setup_inputs(seed: int=0):
    np.random.seed(seed)
    _w = jnp.asarray

    def _L0_attn_setup():
        import jax, jax.numpy as jnp
        import numpy as np
        from jax import lax
        B, L, H = (2, 128, 256)
        E, N, TR, K = (512, 16, 128, 4)
        key = jax.random.key(seed)
        ks = jax.random.split(key, 10)
        s = lambda d: 1.0 / np.sqrt(d)
        return {'input_states': jax.random.normal(ks[0], (B, L, H), jnp.float32), 'W_in': jax.random.normal(ks[1], (H, 2 * E), jnp.float32) * s(H), 'conv_kernel': jax.random.normal(ks[2], (E, 1, K), jnp.float32) * s(K), 'conv_bias': jax.random.normal(ks[3], (E,), jnp.float32) * 0.01, 'W_x': jax.random.normal(ks[4], (E, TR + 2 * N), jnp.float32) * s(E), 'W_dt': jax.random.normal(ks[5], (TR, E), jnp.float32) * s(TR), 'b_dt': jax.random.normal(ks[6], (E,), jnp.float32) * 0.01, 'W_out': jax.random.normal(ks[7], (E, H), jnp.float32) * s(E), 'A_log': jax.random.uniform(ks[8], (E, N), jnp.float32, 0.0, 2.0), 'D': jax.random.normal(ks[9], (E,), jnp.float32)}
    _L0_attn_in = _L0_attn_setup()

    def _L0_ffn_setup():
        import jax, jax.numpy as jnp
        import numpy as np
        B, S, H, E, K, I = (2, 128, 256, 32, 8, 96)
        key = jax.random.key(seed)
        ks = jax.random.split(key, 5)
        scaled = lambda k, shp, fan: jax.random.normal(k, shp, jnp.float32) * fan ** (-0.5)
        return {'hidden_states': jax.random.normal(ks[0], (B, S, H), jnp.float32), 'router_w': scaled(ks[1], (E, H), H), 'w_gate': scaled(ks[2], (E, H, I), H), 'w_up': scaled(ks[3], (E, H, I), H), 'w_down': scaled(ks[4], (E, I, H), I)}
    _L0_ffn_in = _L0_ffn_setup()
    _d = {'L0_attn_input_states': _L0_attn_in['input_states'], 'L0_attn_W_in': _L0_attn_in['W_in'], 'L0_attn_conv_kernel': _L0_attn_in['conv_kernel'], 'L0_attn_conv_bias': _L0_attn_in['conv_bias'], 'L0_attn_W_x': _L0_attn_in['W_x'], 'L0_attn_W_dt': _L0_attn_in['W_dt'], 'L0_attn_b_dt': _L0_attn_in['b_dt'], 'L0_attn_W_out': _L0_attn_in['W_out'], 'L0_attn_A_log': _L0_attn_in['A_log'], 'L0_attn_D': _L0_attn_in['D'], 'L0_ffn_router_w': _L0_ffn_in['router_w'], 'L0_ffn_w_gate': _L0_ffn_in['w_gate'], 'L0_ffn_w_up': _L0_ffn_in['w_up'], 'L0_ffn_w_down': _L0_ffn_in['w_down']}
    _x0 = _d['L0_attn_input_states']
    _d['L0_attn_input_states'] = jax.random.normal(jax.random.fold_in(jax.random.key(seed), 1), (16, 256, 256), dtype=_x0.dtype)
    del _x0
    return _d

def reference(L0_attn_input_states, L0_attn_W_in, L0_attn_conv_kernel, L0_attn_conv_bias, L0_attn_W_x, L0_attn_W_dt, L0_attn_b_dt, L0_attn_W_out, L0_attn_A_log, L0_attn_D, L0_ffn_router_w, L0_ffn_w_gate, L0_ffn_w_up, L0_ffn_w_down):

    def _L0_attn_ref(input_states, W_in, conv_kernel, conv_bias, W_x, W_dt, b_dt, W_out, A_log, D):
        import jax, jax.numpy as jnp
        import numpy as np
        from jax import lax
        B, L, H = (2, 128, 256)
        E, N, TR, K = (512, 16, 128, 4)
        b, l, _ = input_states.shape
        dtype = input_states.dtype
        proj = jnp.einsum('blh,he->bel', input_states, W_in)
        hidden, gate = jnp.split(proj, 2, axis=1)
        x = lax.conv_general_dilated(hidden, conv_kernel, window_strides=(1,), padding=((K - 1, K - 1),), feature_group_count=E)[..., :l]
        hidden = jax.nn.silu(x + conv_bias[None, :, None])
        hs_ble = hidden.transpose(0, 2, 1)
        ssm_p = jnp.einsum('ble,ed->bld', hs_ble, W_x)
        dt, Bm, Cm = jnp.split(ssm_p, [TR, TR + N], axis=-1)
        dts = jax.nn.softplus(jnp.einsum('blr,re->ble', dt, W_dt) + b_dt)
        A = -jnp.exp(A_log.astype(jnp.float32))
        dA = jnp.exp(dts[..., None] * A[None, None])
        dBu = dts[..., None] * Bm[:, :, None, :] * hs_ble[..., None]

        def step(state, inp):
            a, bu, c = inp
            state = a * state + bu
            y = jnp.einsum('ben,bn->be', state.astype(dtype), c)
            return (state, y)
        init = jnp.zeros((b, E, N), dtype=dtype)
        _, ys = lax.scan(step, init, (dA.transpose(1, 0, 2, 3), dBu.transpose(1, 0, 2, 3), Cm.transpose(1, 0, 2)))
        scan_out = ys.transpose(1, 2, 0)
        y = (scan_out + hidden * D[None, :, None]) * jax.nn.silu(gate)
        return jnp.einsum('bel,eh->blh', y, W_out)

    def _L0_ffn_ref(hidden_states, router_w, w_gate, w_up, w_down):
        import jax, jax.numpy as jnp
        import numpy as np
        B, S, H, E, K, I = (2, 128, 256, 32, 8, 96)
        Bq, Sq, Hd = hidden_states.shape
        x = hidden_states.reshape(-1, Hd)
        logits = x @ router_w.T
        probs = jax.nn.softmax(logits.astype(jnp.float32), axis=-1)
        rw, sel = jax.lax.top_k(probs, K)
        rw = rw / jnp.sum(rw, axis=-1, keepdims=True)
        rw = rw.astype(x.dtype)

        def body(acc, operand):
            e, wg, wu, wd = operand
            w_e = jnp.sum(jnp.where(sel == e, rw, jnp.zeros_like(rw)), axis=-1)
            h = jax.nn.silu(x @ wg) * (x @ wu)
            return (acc + h @ wd * w_e[:, None], None)
        acc0 = jnp.zeros_like(x)
        acc, _ = jax.lax.scan(body, acc0, (jnp.arange(E), w_gate, w_up, w_down))
        return acc.reshape(Bq, Sq, Hd)
    x = L0_attn_input_states
    xn = _layernorm(x, axis=-1)
    x = x + _L0_attn_ref(xn, L0_attn_W_in, L0_attn_conv_kernel, L0_attn_conv_bias, L0_attn_W_x, L0_attn_W_dt, L0_attn_b_dt, L0_attn_W_out, L0_attn_A_log, L0_attn_D) + _L0_ffn_ref(xn, L0_ffn_router_w, L0_ffn_w_gate, L0_ffn_w_up, L0_ffn_w_down)
    return x

_drawn_inputs = setup_inputs


def setup_inputs(seed=0):
    import zlib

    import numpy as np

    out = dict(_drawn_inputs(seed))
    spreads = {}
    factors = {'L0_attn_conv_bias': 8.0, 'L0_attn_b_dt': 22.201}
    for name, (base, spread) in spreads.items():
        noise = np.random.default_rng([zlib.crc32(name.encode()), seed]).standard_normal(out[name].shape)
        drawn = base * np.exp(spread * noise) if base else spread * noise
        out[name] = jnp.asarray(drawn.astype(out[name].dtype))
    for name, factor in factors.items():
        out[name] = (out[name] * factor).astype(out[name].dtype)
    return out
```

```python
from contextlib import ExitStack

import concourse.bass as bass
from concourse import mybir

F32 = mybir.dt.float32
ALU = mybir.AluOpType
ACT = mybir.ActivationFunctionType
AX_X = mybir.AxisListType.X
P = 128


def build(nc, x_d, w_in_d, conv_k_d, conv_b_d, w_x_d, w_dt_d, b_dt_d, w_out_d, a_log_d, d_d,
          router_d, w_gate_d, w_up_d, w_down_d, out_d):
    BLOCKS, T, H = x_d.shape
    E, NS = a_log_d.shape
    TAPS = conv_k_d.shape[2]
    R = w_dt_d.shape[0]
    X, _, U = w_gate_d.shape
    TT, HT, ET = T // P, H // P, E // P
    UT = X * U // P
    PAIRS = UT // 2
    TOPK = 8
    assert (TT, HT, ET, R, NS) == (2, 2, 4, P, 16) and BLOCKS % 2 == 0 and UT == 24

    PAIR_AT = [s for s in range(NS) if s % 4 != 1]
    assert len(PAIR_AT) == PAIRS
    FRONT = ["xnT", "logits", "hid0", "hid1", "gate0", "gate1", "weightsT", "low", "C", "dt0", "dt1"]
    READER = {"logits": "V", "gate0": "V", "gate1": "V"}
    NA = sum(READER.get(k, "A") == "A" for k in FRONT)
    NV = len(FRONT) - NA
    FRONT_AT = {s + 1: k for s, k in enumerate(FRONT)}
    GROUP = 3
    GROUPS = PAIRS // GROUP
    BCH = 4
    PIECES = []
    for e in range(4):
        for t in range(3):
            lo, hi = max(e * U, t * P), min((e + 1) * U, (t + 1) * P)
            if lo < hi:
                PIECES.append((t, lo - t * P, hi - t * P, e))
    TRI = 2 * GROUP // 3

    with ExitStack() as ctx:
        def sb(name, shape):
            return ctx.enter_context(nc.sbuf_tensor(name, shape, F32))

        def pb(name, shape):
            return ctx.enter_context(nc.psum_tensor(name, shape, F32))

        def sem(name):
            return ctx.enter_context(nc.semaphore(name))

        w_gate = sb("w_gate", [P, HT, UT * P])
        w_up = sb("w_up", [P, HT, UT * P])
        w_down = sb("w_down", [P, UT, H])
        w_in = sb("w_in", [P, HT, 2 * E])
        w_x = sb("w_x", [P, ET, R + 2 * NS])
        w_dt = sb("w_dt", [P, E])
        w_out = sb("w_out", [P, ET, H])
        router = sb("router", [P, HT, X])
        router_rows = sb("router_rows", [X, H])
        ident = sb("ident", [P, P])
        neg_a = sb("neg_a", [P, ET, NS])
        conv_k = sb("conv_k", [P, ET, TAPS])
        conv_b = sb("conv_b", [P, ET])
        b_dt = sb("b_dt", [P, ET])
        d_half = sb("d_half", [P, ET])
        x_in = sb("x_in", [P, TT, H])
        stats = sb("stats", [P, TT, 6])
        moments = sb("moments", [P, TT, 2])
        var_eps = sb("var_eps", [P, TT])
        minus_half = sb("minus_half", [P, TT])
        eps = sb("eps", [P, TT])
        rstd = sb("rstd", [P, TT])
        xn = sb("xn", [P, TT, H])
        xnT = sb("xnT", [P, 2, HT, T])
        lmax = sb("lmax", [P, TT])
        logit = sb("logit", [P, TT, X])
        expl = sb("expl", [P, TT, X])
        top = sb("top", [P, TT, TOPK])
        rest = sb("rest", [P, TT, X])
        topsum = sb("topsum", [P, TT])
        inv = sb("inv", [P, TT])
        rw = sb("rw", [P, TT, X])
        rwT = sb("rwT", [X, T])
        hp = sb("hp", [P, ET, T + TAPS - 1])
        conv = sb("conv", [P, ET, T])
        tmp = sb("tmp", [P, ET, T])
        u2 = sb("u2", [P, 2, ET, T])
        gate2 = sb("gate2", [P, 2, ET, T])
        dt = sb("dt", [P, 2, ET, T])
        du2 = sb("du2", [P, 2, ET, T])
        low = sb("low", [P, T])
        bcT = sb("bcT", [2 * NS, T])
        c_tok = sb("c_tok", [P, 2, TT, 2 * NS])
        b_rep = sb("b_rep", [P, NS, T])
        rw_rep = sb("rw_rep", [P, 2, 2 * GROUP, T])
        decay = sb("decay", [P, 2, ET, T])
        state = sb("state", [P, 2, ET, T])
        acc = sb("acc", [P, TT, E])
        moe = sb("moe", [P, 3, 2, T])
        res = sb("res", [P, TT, H])

        pair_ps = pb("pair_ps", [P, 2, 2, 2, T])
        turn_ps = pb("turn_ps", [P, TT, E])
        out_ps = pb("out_ps", [P, TT, H])
        front_ps = pb("front_ps", [P, 2, T])

        rw_dram = nc.dram_tensor("rw_dram", [2, X, T], F32).ap()
        b_dram = nc.dram_tensor("b_dram", [2, NS, T], F32).ap()

        w_small_loaded = sem("w_small_loaded")
        w_front_loaded = sem("w_front_loaded")
        w_pair_loaded = sem("w_pair_loaded")
        w_late_loaded = sem("w_late_loaded")
        zeroed = sem("zeroed")
        started = sem("started")
        ident_ready = sem("ident_ready")
        router_turned = sem("router_turned")
        router_ready = sem("router_ready")
        a_exp = sem("a_exp")
        a_ready = sem("a_ready")
        x_loaded = sem("x_loaded")
        stats_ready = sem("stats_ready")
        moments_ready = sem("moments_ready")
        var_ready = sem("var_ready")
        rstd_ready = sem("rstd_ready")
        xn_ready = sem("xn_ready")
        front_filled = sem("front_filled")
        front_read_a = sem("front_read_a")
        front_read_v = sem("front_read_v")
        lmax_ready = sem("lmax_ready")
        expl_ready = sem("expl_ready")
        top_ready = sem("top_ready")
        rw_step = sem("rw_step")
        rw_ready = sem("rw_ready")
        rw_stored = sem("rw_stored")
        b_stored = sem("b_stored")
        gate_tanh = sem("gate_tanh")
        gate_ready = sem("gate_ready")
        conv_step = sem("conv_step")
        conv_tanh = sem("conv_tanh")
        u2_ready = sem("u2_ready")
        z_ready = sem("z_ready")
        nabs_ready = sem("nabs_ready")
        soft_step = sem("soft_step")
        dt_ready = sem("dt_ready")
        du_ready = sem("du_ready")
        b_loaded = [sem(f"b_loaded{c}") for c in range(NS // BCH)]
        rw_loaded = [sem(f"rw_loaded{g}") for g in range(2)]
        decay_ready = sem("decay_ready")
        b_ready = sem("b_ready")
        scanned = sem("scanned")
        turned = sem("turned")
        added = sem("added")
        pair_filled = sem("pair_filled")
        pair_tanh = sem("pair_tanh")
        pair_mul = sem("pair_mul")
        pair_ready = sem("pair_ready")
        pair_used = sem("pair_used")
        y_turned = sem("y_turned")
        y_step = sem("y_step")
        y_ready = sem("y_ready")
        out_filled = sem("out_filled")
        res_loaded = sem("res_loaded")
        res_ready = sem("res_ready")
        stored = sem("stored")

        def wait_alone(eng, signal, value):
            if not isinstance(value, int):
                eng.wait_ge(started, 1)
            eng.wait_ge(signal, value)

        def act_reads(k):
            return sum(READER.get(f, "A") == "A" for f in FRONT[:k])

        def blocks(eng, body):
            body(0, 0, True, False)
            with eng.Fori(0, (BLOCKS - 2) // 2) as g:
                body(2 * g + 1, 1, False, False)
                body(2 * g + 2, 0, False, False)
            body(BLOCKS - 1, 1, False, True)

        block = ctx.enter_context(nc.Block())

        @block.sync
        def _(sp):
            def tokens(dram, i):
                return dram[i, :, :] if isinstance(i, int) else dram[bass.ds(i, 1), :, :].rearrange("o t h -> (o t) h")

            def load_x(i):
                sp.dma_start(x_in[:, :, :], tokens(x_d, i).rearrange("(c p) h -> p c h", p=P)).then_inc(x_loaded, 16)

            def load_res(i):
                sp.dma_start(res[:, :, :], tokens(x_d, i).rearrange("(c p) h -> p c h", p=P)).then_inc(res_loaded, 16)

            def load_rw(i, q, group):
                for t, lo, hi, e in PIECES:
                    dst = rw_rep[lo:hi, group % 2, t::3, :]
                    first = group * TRI * 4 + e
                    src = rw_dram[q, first:first + 4 * (TRI - 1) + 1:4, :]
                    sp.dma_start(dst, src[None, :, :].broadcast_to([hi - lo, TRI, T])).then_inc(rw_loaded[group % 2], 16)

            def load_b(q, c):
                src = b_dram[q, c * BCH:(c + 1) * BCH, :]
                sp.dma_start(b_rep[:, c * BCH:(c + 1) * BCH, :], src[None, :, :].broadcast_to([P, BCH, T])).then_inc(b_loaded[c], 16)

            load_x(0)
            sp.dma_start(router_rows[:, :], router_d).then_inc(w_small_loaded, 16)
            sp.dma_start(neg_a[:, :, :], a_log_d.rearrange("(c p) n -> p c n", p=P)).then_inc(w_small_loaded, 16)
            sp.dma_start(conv_k[:, :, :], conv_k_d.rearrange("(c p) o k -> p c (o k)", p=P)).then_inc(w_small_loaded, 16)
            for dst, src in ((conv_b, conv_b_d), (b_dt, b_dt_d), (d_half, d_d)):
                sp.dma_start(dst[:, :], src.rearrange("(c p) -> p c", p=P), allow_slow_non_contiguous=True).then_inc(w_small_loaded, 16)
            sp.dma_start(w_in[:, :, :], w_in_d.rearrange("(k p) e -> p k e", p=P)).then_inc(w_front_loaded, 16)
            sp.dma_start(w_x[:, :, :], w_x_d.rearrange("(k p) e -> p k e", p=P)).then_inc(w_front_loaded, 16)
            sp.dma_start(w_dt[:, :], w_dt_d).then_inc(w_front_loaded, 16)
            for k in range(HT):
                for dst, src in ((w_gate, w_gate_d), (w_up, w_up_d)):
                    sp.dma_start(dst[:, k, :].rearrange("p (e i) -> p e i", e=X),
                                 src[:, k * P:(k + 1) * P, :].rearrange("e p i -> p e i")).then_inc(w_pair_loaded, 16)
            sp.dma_start(w_down[:, :, :], w_down_d.rearrange("e i h -> (e i) h").rearrange("(j p) h -> p j h", p=P)).then_inc(w_late_loaded, 16)
            sp.dma_start(w_out[:, :, :], w_out_d.rearrange("(k p) h -> p k h", p=P)).then_inc(w_late_loaded, 16)

            sp.wait_ge(xn_ready, 1)
            load_x(1)
            sp.wait_ge(rw_stored, 16)
            load_rw(0, 0, 0)
            load_rw(0, 0, 1)
            sp.wait_ge(b_stored, 16)
            for c in range(NS // BCH):
                load_b(0, c)

            def store(i):
                wait_alone(sp, res_ready, i + 1)
                sp.dma_start(tokens(out_d, i).rearrange("(c p) h -> p c h", p=P), res[:, :, :]).then_inc(stored, 16)

            def residual(i, first):
                if not first:
                    wait_alone(sp, stored, i * 16)
                load_res(i)

            def main(i, q, first, last, ahead):
                if ahead:
                    sp.wait_ge(x_loaded, (i + 2) * 16)
                    sp.wait_ge(xn_ready, i + 2)
                    load_x(i + 2)
                if not first:
                    store(i - 1)
                    residual(i, False)
                else:
                    residual(0, True)
                for group in (2, 3):
                    sp.wait_ge(pair_ready, i * PAIRS + (group - 1) * GROUP)
                    load_rw(i, q, group)
                if last:
                    return
                wait_alone(sp, rw_stored, (i + 2) * 16)
                sp.wait_ge(pair_ready, i * PAIRS + 3 * GROUP)
                load_rw(i + 1, 1 - q, 0)
                wait_alone(sp, b_stored, (i + 2) * 16)
                for c in range(NS // BCH):
                    sp.wait_ge(b_ready, i * NS + (c + 1) * BCH)
                    load_b(1 - q, c)
                sp.wait_ge(pair_ready, (i + 1) * PAIRS)
                load_rw(i + 1, 1 - q, 1)

            main(0, 0, True, False, True)
            with sp.Fori(0, (BLOCKS - 2) // 2 - 1) as g:
                main(2 * g + 1, 1, False, False, True)
                main(2 * g + 2, 0, False, False, True)
            main(BLOCKS - 3, 1, False, False, True)
            main(BLOCKS - 2, 0, False, False, False)
            main(BLOCKS - 1, 1, False, True, False)
            store(BLOCKS - 1)
            sp.wait_ge(stored, BLOCKS * 16)
            sp.wait_ge(rw_stored, BLOCKS * 16)
            sp.wait_ge(b_stored, BLOCKS * 16)

        @block.gpsimd
        def _(pool):
            pool.memset(minus_half[:, :], -0.5).then_inc(started, 1)
            pool.memset(eps[:, :], 1e-5).then_inc(started, 1)
            pool.memset(ident[:, :], 0.0).then_inc(zeroed, 1)
            pool.memset(hp[:, :, 0:TAPS - 1], 0.0).then_inc(zeroed, 1)
            pool.memset(decay[:, :, :, 0:1], 0.0).then_inc(zeroed, 1)
            pool.wait_ge(zeroed, 1)
            pool.affine_select(out=ident[:, :], in_=ident[:, :], compare_op=ALU.not_equal, fill=1.0, base=0,
                               pattern=[[-1, P]], channel_multiplier=1).then_inc(ident_ready, 1)

            def norm(i):
                pool.wait_ge(started, 2)
                pool.wait_ge(moments_ready, i + 1)
                pool.tensor_tensor(var_eps[:, :], moments[:, :, 1], eps[:, :], ALU.add).then_inc(var_ready, 1)
                pool.wait_ge(var_ready, i + 1)
                pool.tensor_tensor(rstd[:, :], var_eps[:, :], minus_half[:, :], ALU.pow).then_inc(rstd_ready, 1)

            def step_input(i, q):
                pool.wait_ge(dt_ready, i + 1)
                pool.tensor_tensor(du2[:, q, :, :], u2[:, q, :, :], dt[:, q, :, :], ALU.mult).then_inc(du_ready, 1)

            def state_input(i, q, n, m):
                if n == 0:
                    pool.wait_ge(du_ready, i + 1)
                if n % BCH == 0:
                    pool.wait_ge(b_loaded[n // BCH], (i + 1) * 16)
                if not (isinstance(i, int) and i == 0 and n < 2):
                    pool.wait_ge(turned, i * NS + n - 1)
                pool.tensor_tensor(state[:, m, :, :], du2[:, q, :, :],
                                   b_rep[:, n, :][:, None, :].broadcast_to([P, ET, T]), ALU.mult).then_inc(b_ready, 1)

            def weigh(i, p):
                if p % GROUP == 0:
                    group = p // GROUP
                    pool.wait_ge(rw_loaded[group % 2], (i * (GROUPS // 2) + group // 2 + 1) * 16 * len(PIECES))
                pool.wait_ge(pair_mul, i * PAIRS + p + 1)
                k = 2 * (p % GROUP)
                pool.tensor_tensor(moe[:, p % 3, :, :], moe[:, p % 3, :, :],
                                   rw_rep[:, (p // GROUP) % 2, k:k + 2, :], ALU.mult).then_inc(pair_ready, 1)

            norm(0)
            step_input(0, 0)
            state_input(0, 0, 0, 0)

            def main(i, q, first, last):
                for s in range(NS):
                    if s < NS - 1:
                        state_input(i, q, s + 1, (s + 1) % 2)
                    elif not last:
                        state_input(i + 1, 1 - q, 0, 0)
                    if s in PAIR_AT:
                        weigh(i, PAIR_AT.index(s))
                    if not last and s == 0:
                        norm(i + 1)
                    if not last and s == 13:
                        step_input(i + 1, 1 - q)

            blocks(pool, main)

        @block.scalar
        def _(act):
            act.wait_ge(w_small_loaded, 6 * 16)
            act.activation(neg_a[:, :, :], neg_a[:, :, :], ACT.Exp).then_inc(a_exp, 1)
            act.wait_ge(router_turned, 1)
            act.activation(router[:, :, :], front_ps[:, 0, 0:HT * X].rearrange("p (k e) -> p k e", k=HT), ACT.Copy).then_inc(router_ready, 1)

            def decays(i, q, n, m):
                if n == 0:
                    act.wait_ge(dt_ready, i + 1)
                if isinstance(i, int) and i == 0 and n < 2:
                    act.wait_ge(zeroed, 3)
                else:
                    act.wait_ge(scanned, i * NS + n - 1)
                for e in range(ET):
                    last = act.activation(decay[:, m, e, 1:T], dt[:, q, e, 1:T], ACT.Exp, scale=neg_a[:, e, n:n + 1])
                last.then_inc(decay_ready, 1)

            def pair(i, p):
                act.wait_ge(pair_filled, i * PAIRS + p + 1)
                if not (isinstance(i, int) and i == 0 and p < 3):
                    act.wait_ge(pair_used, i * PAIRS + p - 2)
                act.activation(moe[:, p % 3, :, :], pair_ps[:, p % 2, 0, :, :], ACT.Tanh, scale=0.5).then_inc(pair_tanh, 1)

            def front(k, i, q):
                name = FRONT[k]
                act.wait_ge(front_filled, i * len(FRONT) + k + 1)
                if name == "xnT":
                    act.activation(xnT[:, q, :, :], front_ps[:, :, :], ACT.Copy).then_inc(front_read_a, 1)
                elif name in ("hid0", "hid1"):
                    e = 2 * (name == "hid1")
                    if name == "hid0":
                        act.wait_ge(zeroed, 3)
                    if not (isinstance(i, int) and i == 0):
                        act.wait_ge(conv_step, i * 3)
                    act.activation(hp[:, e:e + 2, TAPS - 1:], front_ps[:, :, :], ACT.Copy).then_inc(front_read_a, 1)
                elif name in ("gate0", "gate1"):
                    e = 2 * (name == "gate1")
                    act.activation(gate2[:, q, e:e + 2, :], front_ps[:, :, :], ACT.Tanh, scale=0.5).then_inc(gate_tanh, 1)
                elif name == "weightsT":
                    if not (isinstance(i, int) and i == 0):
                        act.wait_ge(rw_stored, i * 16)
                    act.activation(rwT[:, :], front_ps[0:X, 0, :], ACT.Copy).then_inc(front_read_a, 1)
                    act.wait_ge(front_read_a, i * NA + act_reads(k) + 1)
                    act.dma_start(rw_dram[q, :, :], rwT[:, :]).then_inc(rw_stored, 16)
                elif name == "low":
                    if not (isinstance(i, int) and i == 0):
                        act.wait_ge(b_stored, i * 16)
                    act.activation(bcT[:, :], front_ps[0:2 * NS, 1, :], ACT.Copy, scale=0.5)
                    act.activation(low[:, :], front_ps[:, 0, :], ACT.Copy, scale=0.5).then_inc(front_read_a, 1)
                    act.wait_ge(front_read_a, i * NA + act_reads(k) + 1)
                    act.dma_start(b_dram[q, :, :], bcT[0:NS, :]).then_inc(b_stored, 16)
                elif name == "C":
                    act.activation(c_tok[:, q, :, :], front_ps[:, 0, 0:TT * 2 * NS].rearrange("p (t n) -> p t n", t=TT),
                                   ACT.Copy, scale=0.5).then_inc(front_read_a, 1)
                elif name in ("dt0", "dt1"):
                    e = 2 * (name == "dt1")
                    for j in range(2):
                        last = act.activation(conv[:, e + j, :], front_ps[:, j, :], ACT.Identity, bias=b_dt[:, e + j:e + j + 1])
                    last.then_inc(front_read_a, 1)

            def router_exp(i):
                act.wait_ge(lmax_ready, i * 2 + 2)
                act.activation(expl[:, :, :], logit[:, :, :], ACT.Exp).then_inc(expl_ready, 1)

            def conv_first(i):
                act.wait_ge(front_read_a, i * NA + act_reads(FRONT.index("hid1")) + 1)
                if not (isinstance(i, int) and i == 0):
                    act.wait_ge(dt_ready, i)
                for e in range(ET):
                    last = act.activation(conv[:, e, :], hp[:, e, 0:T], ACT.Identity, bias=conv_b[:, e:e + 1], scale=conv_k[:, e, 0:1])
                last.then_inc(z_ready, 1)

            def conv_silu(i):
                act.wait_ge(conv_step, i * 3 + 3)
                act.activation(tmp[:, :, :], conv[:, :, :], ACT.Tanh, scale=0.5).then_inc(conv_tanh, 1)

            def softplus(i):
                act.wait_ge(nabs_ready, i + 1)
                act.activation(tmp[:, :, :], tmp[:, :, :], ACT.Exp).then_inc(soft_step, 1)
                act.wait_ge(soft_step, 2 * i + 1)
                act.activation(tmp[:, :, :], tmp[:, :, :], ACT.Ln, bias=1.0).then_inc(soft_step, 1)

            def front_at(s, i, q):
                if s in FRONT_AT:
                    front(s - 1, i, q)
                if s == 3:
                    router_exp(i)
                if s == 4:
                    conv_first(i)
                if s == 6:
                    conv_silu(i)
                if s == 12:
                    softplus(i)

            for s in range(NS):
                front_at(s, 0, 0)
            decays(0, 0, 0, 0)

            def main(i, q, first, last):
                for s in range(NS):
                    if s < NS - 1:
                        decays(i, q, s + 1, (s + 1) % 2)
                    elif not last:
                        decays(i + 1, 1 - q, 0, 0)
                    if s in PAIR_AT:
                        pair(i, PAIR_AT.index(s))
                    if not last:
                        front_at(s, i + 1, 1 - q)

            blocks(act, main)

        @block.vector
        def _(dve):
            dve.wait_ge(a_exp, 1)
            dve.tensor_scalar(neg_a[:, :, :], neg_a[:, :, :], -1.0, None, ALU.mult).then_inc(a_ready, 1)
            dve.tensor_scalar(d_half[:, :], d_half[:, :], 0.5, None, ALU.mult).then_inc(a_ready, 1)

            def norm(i):
                dve.wait_ge(x_loaded, (i + 1) * 16)
                for c in range(TT):
                    last = dve.bn_stats(stats[:, c, :], x_in[:, c, :])
                last.then_inc(stats_ready, 1)
                wait_alone(dve, stats_ready, i + 1)
                for c in range(TT):
                    last = dve.bn_aggr(moments[:, c, :], stats[:, c, :])
                last.then_inc(moments_ready, 1)

            def normed(i):
                dve.wait_ge(rstd_ready, i + 1)
                if not (isinstance(i, int) and i == 0):
                    dve.wait_ge(front_filled, (i - 1) * len(FRONT) + 1)
                for c in range(TT):
                    last = dve.tensor_scalar(xn[:, c, :], x_in[:, c, :], moments[:, c, 0:1], rstd[:, c:c + 1],
                                             ALU.subtract, ALU.mult)
                last.then_inc(xn_ready, 1)

            def logits(i):
                ps = front_ps[:, 0, 0:TT * X].rearrange("p (t e) -> p t e", t=TT)
                dve.wait_ge(front_filled, i * len(FRONT) + FRONT.index("logits") + 1)
                dve.tensor_reduce(lmax[:, :], ps, AX_X, ALU.max).then_inc(lmax_ready, 1)
                dve.wait_ge(lmax_ready, 2 * i + 1)
                dve.tensor_tensor(logit[:, :, :], ps, lmax[:, :, None].broadcast_to([P, TT, X]), ALU.subtract).then_inc(lmax_ready, 1)

            def route(i):
                wait_alone(dve, expl_ready, i + 1)
                for c in range(TT):
                    last = dve.max(top[:, c, :], expl[:, c, :])
                last.then_inc(top_ready, 1)
                wait_alone(dve, top_ready, i + 1)
                for c in range(TT):
                    dve.match_replace(rest[:, c, :], top[:, c, :], expl[:, c, :], -1.0)
                dve.tensor_reduce(topsum[:, :], top[:, :, :], AX_X, ALU.add).then_inc(rw_step, 1)
                dve.wait_ge(rw_step, 3 * i + 1)
                dve.reciprocal(inv[:, :], topsum[:, :]).then_inc(rw_step, 1)
                dve.scalar_tensor_tensor(out=rest[:, :, :], in0=rest[:, :, :], scalar=0.0, in1=expl[:, :, :],
                                         op0=ALU.is_lt, op1=ALU.mult).then_inc(rw_step, 1)
                dve.wait_ge(rw_step, 3 * i + 3)
                if not (isinstance(i, int) and i == 0):
                    dve.wait_ge(front_filled, (i - 1) * len(FRONT) + FRONT.index("weightsT") + 1)
                dve.scalar_tensor_tensor(out=rw[:, :, :], in0=rest[:, :, :], scalar=0.5,
                                         in1=inv[:, :, None].broadcast_to([P, TT, X]), op0=ALU.mult, op1=ALU.mult).then_inc(rw_ready, 1)

            def gate(i, q, k):
                name = FRONT[k]
                e = 2 * (name == "gate1")
                dve.wait_ge(gate_tanh, 2 * i + e // 2 + 1)
                dve.scalar_tensor_tensor(out=gate2[:, q, e:e + 2, :], in0=gate2[:, q, e:e + 2, :], scalar=1.0,
                                         in1=front_ps[:, :, :], op0=ALU.add, op1=ALU.mult).then_inc(front_read_v, 1)

            def taps(i):
                dve.wait_ge(z_ready, i + 1)
                for k in range(1, TAPS):
                    if k > 1:
                        dve.wait_ge(conv_step, 3 * i + k - 1)
                    for e in range(ET):
                        last = dve.scalar_tensor_tensor(out=conv[:, e, :], in0=hp[:, e, k:k + T], scalar=conv_k[:, e, k:k + 1],
                                                        in1=conv[:, e, :], op0=ALU.mult, op1=ALU.add)
                    last.then_inc(conv_step, 1)

            def silu(i, q):
                dve.wait_ge(conv_tanh, i + 1)
                dve.scalar_tensor_tensor(out=u2[:, q, :, :], in0=tmp[:, :, :], scalar=1.0, in1=conv[:, :, :],
                                         op0=ALU.add, op1=ALU.mult).then_inc(u2_ready, 1)

            def minus_abs(i):
                dve.wait_ge(front_read_a, (i + 1) * NA)
                dve.scalar_tensor_tensor(out=tmp[:, :, :], in0=conv[:, :, :], scalar=-1.0, in1=conv[:, :, :],
                                         op0=ALU.mult, op1=ALU.min).then_inc(nabs_ready, 1)

            def steps(i, q):
                dve.wait_ge(soft_step, 2 * i + 2)
                dve.scalar_tensor_tensor(out=dt[:, q, :, :], in0=conv[:, :, :], scalar=0.0, in1=tmp[:, :, :],
                                         op0=ALU.max, op1=ALU.add).then_inc(dt_ready, 1)

            def scan(i, n, m):
                dve.wait_ge(decay_ready, i * NS + n + 1)
                dve.wait_ge(b_ready, i * NS + n + 1)
                h = state[:, m, :, :].rearrange("p e t -> p (e t)")
                dve.tensor_tensor_scan(h, decay[:, m, :, :].rearrange("p e t -> p (e t)"), h, 0.0,
                                       ALU.mult, ALU.add).then_inc(scanned, 1)

            def add_state(i, q, n):
                for c in range(TT):
                    dve.wait_ge(turned, i * NS + n + 1)
                    scale = c_tok[:, q, c, NS + n:NS + n + 1]
                    if n == 0:
                        if not (isinstance(i, int) and i == 0):
                            dve.wait_ge(y_turned, i)
                        last = dve.tensor_scalar(acc[:, c, :], turn_ps[:, c, :], scale, None, ALU.mult)
                    else:
                        dve.wait_ge(added, i * NS + n)
                        last = dve.scalar_tensor_tensor(out=acc[:, c, :], in0=turn_ps[:, c, :], scalar=scale,
                                                        in1=acc[:, c, :], op0=ALU.mult, op1=ALU.add)
                last.then_inc(added, 1)

            def pair(i, p):
                dve.wait_ge(pair_tanh, i * PAIRS + p + 1)
                m = moe[:, p % 3, :, :]
                dve.scalar_tensor_tensor(out=m, in0=m, scalar=1.0, in1=pair_ps[:, p % 2, 0, :, :],
                                         op0=ALU.add, op1=ALU.mult).then_inc(y_step, 1)
                dve.wait_ge(y_step, i * PAIRS + p + 1)
                dve.tensor_tensor(m, m, pair_ps[:, p % 2, 1, :, :], ALU.mult).then_inc(pair_mul, 1)

            def gated(i, q):
                dve.wait_ge(y_turned, i + 1)
                for e in range(ET):
                    last = dve.scalar_tensor_tensor(out=u2[:, q, e, :], in0=u2[:, q, e, :], scalar=d_half[:, e:e + 1],
                                                    in1=turn_ps[:, e // 2, (e % 2) * T:(e % 2 + 1) * T], op0=ALU.mult, op1=ALU.add)
                last.then_inc(y_ready, 1)
                dve.wait_ge(y_ready, 2 * i + 1)
                dve.scalar_tensor_tensor(out=u2[:, q, :, :], in0=u2[:, q, :, :], scalar=0.5, in1=gate2[:, q, :, :],
                                         op0=ALU.mult, op1=ALU.mult).then_inc(y_ready, 1)

            def total(i):
                dve.wait_ge(out_filled, i + 1)
                dve.wait_ge(res_loaded, (i + 1) * 16)
                dve.tensor_tensor(res[:, :, :], res[:, :, :], out_ps[:, :, :], ALU.add).then_inc(res_ready, 1)

            def front_at(s, i, q):
                if s == 0:
                    norm(i)
                    normed(i)
                if s == 2:
                    logits(i)
                if s == 3:
                    route(i)
                if s == 5:
                    taps(i)
                    gate(i, q, s - 1)
                if s == 6:
                    gate(i, q, s - 1)
                    silu(i, q)
                if s == 11:
                    minus_abs(i)
                if s == 12:
                    steps(i, q)

            for s in range(NS):
                front_at(s, 0, 0)

            def main(i, q, first, last):
                for s in range(NS):
                    scan(i, s, s % 2)
                    if s == 1 and not first:
                        gated(i - 1, 1 - q)
                    if s > 0:
                        add_state(i, q, s - 1)
                    elif not first:
                        add_state(i - 1, 1 - q, NS - 1)
                    if s in PAIR_AT:
                        pair(i, PAIR_AT.index(s))
                    if s == 2 and not first:
                        total(i - 1)
                    if not last:
                        front_at(s, i + 1, 1 - q)

            blocks(dve, main)
            end = BLOCKS - 1
            add_state(end, 1, NS - 1)
            gated(end, 1)
            total(end)

        @block.tensor
        def _(pe):
            pe.wait_ge(ident_ready, 1)
            pe.wait_ge(w_small_loaded, 6 * 16)
            for k in range(HT):
                last = pe.transpose(front_ps[:, 0, k * X:(k + 1) * X], router_rows[:, k * P:(k + 1) * P], ident[0:X, 0:X])
            last.then_inc(router_turned, 1)

            def front(k, i, q):
                name = FRONT[k]
                before = FRONT[k - 1]
                if not (isinstance(i, int) and i == 0 and k == 0):
                    if k == 0:
                        pe.wait_ge(front_read_a, i * NA)
                    elif before == "logits":
                        pe.wait_ge(lmax_ready, 2 * i + 2)
                    elif before in ("gate0", "gate1"):
                        pe.wait_ge(front_read_v, 2 * i + FRONT[:k].count("gate0") + FRONT[:k].count("gate1"))
                    else:
                        pe.wait_ge(front_read_a, i * NA + act_reads(k))
                else:
                    pe.wait_ge(router_ready, 1)
                if name == "xnT":
                    pe.wait_ge(xn_ready, i + 1)
                    for h in range(HT):
                        for c in range(TT):
                            last = pe.transpose(front_ps[:, h, c * P:(c + 1) * P], xn[:, c, h * P:(h + 1) * P], ident[:, :])
                elif name == "logits":
                    for c in range(TT):
                        for h in range(HT):
                            last = pe.matmul(front_ps[:, 0, c * X:(c + 1) * X], xnT[:, q, h, c * P:(c + 1) * P], router[:, h, :],
                                             start=(h == 0), stop=(h == HT - 1))
                elif name in ("hid0", "hid1", "gate0", "gate1"):
                    if isinstance(i, int) and i == 0:
                        pe.wait_ge(w_front_loaded, 3 * 16)
                    for j in range(2):
                        m = 2 * (k - FRONT.index("hid0")) + j
                        for h in range(HT):
                            last = pe.matmul(front_ps[:, j, :], w_in[:, h, m * P:(m + 1) * P], xnT[:, q, h, :],
                                             start=(h == 0), stop=(h == HT - 1))
                elif name == "weightsT":
                    pe.wait_ge(rw_ready, i + 1)
                    for c in range(TT):
                        last = pe.transpose(front_ps[0:X, 0, c * P:(c + 1) * P], rw[:, c, :], ident[:, :])
                elif name == "low":
                    pe.wait_ge(u2_ready, i + 1)
                    for e in range(ET):
                        last = pe.matmul(front_ps[:, 0, :], w_x[:, e, 0:R], u2[:, q, e, :], start=(e == 0), stop=(e == ET - 1))
                    for e in range(ET):
                        last = pe.matmul(front_ps[0:2 * NS, 1, :], w_x[:, e, R:R + 2 * NS], u2[:, q, e, :],
                                         start=(e == 0), stop=(e == ET - 1))
                elif name == "C":
                    for c in range(TT):
                        last = pe.matmul(front_ps[:, 0, c * 2 * NS:(c + 1) * 2 * NS], bcT[:, c * P:(c + 1) * P],
                                         ident[0:2 * NS, 0:2 * NS], start=True, stop=True)
                elif name in ("dt0", "dt1"):
                    for j in range(2):
                        m = 2 * (name == "dt1") + j
                        last = pe.matmul(front_ps[:, j, :], w_dt[:, m * P:(m + 1) * P], low[:, :], start=True, stop=True)
                last.then_inc(front_filled, 1)

            def turn(i, n, m):
                pe.wait_ge(scanned, i * NS + n + 1)
                if n > 0:
                    pe.wait_ge(added, i * NS + n)
                elif not (isinstance(i, int) and i == 0):
                    pe.wait_ge(y_ready, 2 * i)
                for c in range(TT):
                    for e in range(ET):
                        last = pe.transpose(turn_ps[:, c, e * P:(e + 1) * P], state[:, m, e, c * P:(c + 1) * P], ident[:, :])
                last.then_inc(turned, 1)

            def turn_y(i):
                pe.wait_ge(added, (i + 1) * NS)
                for e in range(ET):
                    for c in range(TT):
                        at = (e % 2) * T + c * P
                        last = pe.transpose(turn_ps[:, e // 2, at:at + P], acc[:, c, e * P:(e + 1) * P], ident[:, :])
                last.then_inc(y_turned, 1)

            def pair_in(i, q, p):
                if isinstance(i, int) and i == 0 and p == 0:
                    pe.wait_ge(w_pair_loaded, 4 * 16)
                if not (isinstance(i, int) and i == 0 and p < 2):
                    pe.wait_ge(pair_mul, i * PAIRS + p - 1)
                for which, w in ((0, w_gate), (1, w_up)):
                    for j in range(2):
                        t = 2 * p + j
                        for h in range(HT):
                            last = pe.matmul(pair_ps[:, p % 2, which, j, :], w[:, h, t * P:(t + 1) * P], xnT[:, q, h, :],
                                             start=(h == 0), stop=(h == HT - 1))
                last.then_inc(pair_filled, 1)

            def pair_out(i, p):
                if isinstance(i, int) and i == 0 and p == 0:
                    pe.wait_ge(w_late_loaded, 2 * 16)
                pe.wait_ge(pair_ready, i * PAIRS + p + 1)
                if p == 0 and not (isinstance(i, int) and i == 0):
                    pe.wait_ge(res_ready, i)
                for j in range(2):
                    for c in range(TT):
                        last = pe.matmul(out_ps[:, c, :], moe[:, p % 3, j, c * P:(c + 1) * P], w_down[:, 2 * p + j, :],
                                         start=(p == 0 and j == 0 and c == 0), stop=False, skip_group_check=True)
                last.then_inc(pair_used, 1)

            def project_y(i, q):
                pe.wait_ge(y_ready, 2 * i + 2)
                for e in range(ET):
                    for c in range(TT):
                        last = pe.matmul(out_ps[:, c, :], u2[:, q, e, c * P:(c + 1) * P], w_out[:, e, :],
                                         start=False, stop=(e == ET - 1), skip_group_check=True)
                last.then_inc(out_filled, 1)

            for k in range(len(FRONT)):
                front(k, 0, 0)

            def main(i, q, first, last):
                for s in range(NS):
                    if s == 1 and not first:
                        turn_y(i - 1)
                    if s in PAIR_AT:
                        p = PAIR_AT.index(s)
                        pair_in(i, q, p)
                        if p >= 2:
                            pair_out(i, p - 2)
                        elif not first:
                            pair_out(i - 1, PAIRS - 2 + p)
                    if s == 2 and not first:
                        project_y(i - 1, 1 - q)
                    if s > 0:
                        turn(i, s - 1, (s - 1) % 2)
                    elif not first:
                        turn(i - 1, NS - 1, 1)
                    if not last and s in FRONT_AT:
                        front(s - 1, i + 1, 1 - q)

            blocks(pe, main)
            end = BLOCKS - 1
            turn(end, NS - 1, 1)
            pair_out(end, PAIRS - 2)
            pair_out(end, PAIRS - 1)
            turn_y(end)
            project_y(end, 1)


_INS = ['L0_attn_input_states', 'L0_attn_W_in', 'L0_attn_conv_kernel', 'L0_attn_conv_bias', 'L0_attn_W_x',
        'L0_attn_W_dt', 'L0_attn_b_dt', 'L0_attn_W_out', 'L0_attn_A_log', 'L0_attn_D', 'L0_ffn_router_w',
        'L0_ffn_w_gate', 'L0_ffn_w_up', 'L0_ffn_w_down']


def kernel(**inputs):
    import numpy as _np
    import concourse.bacc as _bacc
    from concourse import mybir as _mybir
    from concourse.bass_utils import run_bass_kernel_spmd as _run

    nc = _bacc.Bacc("TRN2", target_bir_lowering=False, num_devices=1)
    arrays, args = {}, []
    for name in _INS:
        a = _np.ascontiguousarray(inputs[name])
        arrays[f"in_{name}_dram"] = a
        args.append(nc.dram_tensor(f"in_{name}_dram", a.shape, _mybir.dt.from_np(a.dtype), kind="ExternalInput").ap())
    shape = inputs['L0_attn_input_states'].shape
    args.append(nc.dram_tensor("out_0_dram", shape, _mybir.dt.float32, kind="ExternalOutput").ap())
    build(nc, *args)
    r = _run(nc, [arrays], core_ids=[0])
    return r.results[0]["out_0_dram"]
```

```python
from contextlib import ExitStack

import concourse.bass as bass
from concourse import mybir

F32 = mybir.dt.float32
F32R = mybir.dt.float32r
ALU = mybir.AluOpType
ACT = mybir.ActivationFunctionType
AX_X = mybir.AxisListType.X
P = 128


def build(nc, x_d, w_in_d, conv_k_d, conv_b_d, w_x_d, w_dt_d, b_dt_d, w_out_d, a_log_d, d_d,
          router_d, w_gate_d, w_up_d, w_down_d, out_d):
    BLOCKS, T, H = x_d.shape
    E, NS = a_log_d.shape
    TAPS = conv_k_d.shape[2]
    R = w_dt_d.shape[0]
    X, _, U = w_gate_d.shape
    TT, HT, ET = T // P, H // P, E // P
    UT = X * U // P
    PAIRS = UT // 2
    TOPK = 8
    assert (TT, HT, ET, R, NS) == (2, 2, 4, P, 16) and BLOCKS % 2 == 0 and UT == 24

    def halves(s):
        return range(s * 2 * PAIRS // NS, (s + 1) * 2 * PAIRS // NS)

    PAIR_AT = [s for p in range(PAIRS) for s in range(NS) if 2 * p + 1 in halves(s)]
    FRONT = ["xnT", "logits", "hid0", "hid1", "weightsT", "low", "C", "dt0", "dt1"]
    STEP = {"xnT": 1, "logits": 2, "hid0": 3, "hid1": 4, "weightsT": 6, "low": 9, "C": 10, "dt0": 11, "dt1": 12}
    GATE_STEP = (13, 14)
    NF, NV = len(FRONT), 2
    NA = NF - NV
    BCH = 2
    CHUNKS = NS // BCH
    RING = 3
    WGROUPS = 4

    def pieces(p):
        found = []
        for t in range(2):
            at = (2 * p + t) * P
            for e in range(at // U, (at + P - 1) // U + 1):
                found.append((t, max(e * U - at, 0), min((e + 1) * U - at, P), e))
        return found

    assert all(len(pieces(p)) == 4 for p in range(PAIRS)) and PAIRS % RING == 0

    with ExitStack() as ctx:
        def sb(name, shape, dtype=F32):
            return ctx.enter_context(nc.sbuf_tensor(name, shape, dtype))

        def pb(name, shape):
            return ctx.enter_context(nc.psum_tensor(name, shape, F32))

        def sem(name):
            return ctx.enter_context(nc.semaphore(name))

        w_gate = [sb(f"w_gate_{x}", [P, HT, UT * P], F32R) for x in ("hi", "lo")]
        w_up = [sb(f"w_up_{x}", [P, HT, UT * P], F32R) for x in ("hi", "lo")]
        w_in = [sb(f"w_in_{x}", [P, HT, 2 * E], F32R) for x in ("hi", "lo")]
        router = [sb(f"router_{x}", [P, HT, X], F32R) for x in ("hi", "lo")]
        w_x = sb("w_x", [P, ET, R + 2 * NS])
        w_dt = sb("w_dt", [P, E])
        w_out = sb("w_out", [P, ET, H])
        ident = sb("ident", [P, P])
        neg_a = sb("neg_a", [P, ET, NS])
        conv_k = sb("conv_k", [P, ET, TAPS])
        conv_b = sb("conv_b", [P, ET])
        b_dt = sb("b_dt", [P, ET])
        d_half = sb("d_half", [P, ET])
        x_in = sb("x_in", [P, TT, H])
        stats = sb("stats", [P, TT, 6])
        moments = sb("moments", [P, TT, 2])
        var_eps = sb("var_eps", [P, TT])
        minus_half = sb("minus_half", [P, TT])
        eps = sb("eps", [P, TT])
        rstd = sb("rstd", [P, TT])
        xnT = [sb(f"xnT_{x}", [P, 2, HT, T], F32R) for x in ("hi", "lo")]
        lmax = sb("lmax", [P, TT])
        logit = sb("logit", [P, TT, X])
        expl = sb("expl", [P, TT, X])
        top = sb("top", [P, TT, TOPK])
        rest = sb("rest", [P, TT, X])
        topsum = sb("topsum", [P, TT])
        inv = sb("inv", [P, TT])
        rw = logit
        low = sb("low", [P, T])
        rwT = low[0:X, :]
        bcT = sb("bcT", [2 * NS, T])
        c_tok = sb("c_tok", [P, 2, TT, 2 * NS])
        PAD = TAPS - 1
        u2p = sb("u2p", [P, 2, ET, PAD + T])
        hp = u2p
        u2 = u2p[:, :, :, PAD:]
        dt = sb("dt", [P, 2, ET, T])
        conv = dt
        du2 = sb("du2", [P, 2, ET, T])
        tmp = du2
        gate2 = sb("gate2", [P, ET, T])
        b_rep = sb("b_rep", [P, 2, BCH, T])
        rw_rep = sb("rw_rep", [P, RING, 2, T])
        w_down = sb("w_down", [P, RING, 2, H])
        decay = sb("decay", [P, 2, ET, T])
        state = sb("state", [P, 2, ET, T])
        acc = sb("acc", [P, TT, E])
        moe = sb("moe", [P, RING, 2, T])
        res = sb("res", [P, TT, H])
        staging = [x[:, m, :, :].rearrange("p e t -> p (e t)") for x in (decay, state) for m in range(2)]
        router_rows = acc[0:X, 0, 0:H]

        pair_ps = pb("pair_ps", [P, 2, 2, 2, T])
        turn_ps = pb("turn_ps", [P, TT, E])
        out_ps = pb("out_ps", [P, TT, H])
        front_ps = pb("front_ps", [P, 2, T])

        rw_dram = nc.dram_tensor("rw_dram", [2, X, T], F32).ap()
        b_dram = nc.dram_tensor("b_dram", [2, NS, T], F32).ap()

        w_small_loaded = sem("w_small_loaded")
        w_front_loaded = sem("w_front_loaded")
        w_late_loaded = sem("w_late_loaded")
        staged = [sem(f"staged{k}") for k in range(len(staging))]
        split_hi = sem("split_hi")
        split = sem("split")
        router_hi = sem("router_hi")
        zeroed = sem("zeroed")
        started = sem("started")
        ident_ready = sem("ident_ready")
        router_turned = sem("router_turned")
        router_ready = sem("router_ready")
        a_exp = sem("a_exp")
        a_ready = sem("a_ready")
        x_loaded = sem("x_loaded")
        stats_ready = sem("stats_ready")
        moments_ready = sem("moments_ready")
        var_ready = sem("var_ready")
        rstd_ready = sem("rstd_ready")
        xn_ready = sem("xn_ready")
        front_filled = sem("front_filled")
        front_read_a = sem("front_read_a")
        front_read_v = sem("front_read_v")
        lmax_ready = sem("lmax_ready")
        expl_ready = sem("expl_ready")
        top_ready = sem("top_ready")
        rw_step = sem("rw_step")
        rw_ready = sem("rw_ready")
        rw_stored = sem("rw_stored")
        b_stored = sem("b_stored")
        xnT_hi = sem("xnT_hi")
        gate_filled = sem("gate_filled")
        gate_tanh = sem("gate_tanh")
        gate_read = sem("gate_read")
        conv_step = sem("conv_step")
        conv_tanh = sem("conv_tanh")
        u2_ready = sem("u2_ready")
        z_ready = sem("z_ready")
        nabs_ready = sem("nabs_ready")
        soft_step = sem("soft_step")
        dt_ready = sem("dt_ready")
        du_ready = sem("du_ready")
        b_loaded = [sem(f"b_loaded{c}") for c in range(2)]
        rw_loaded = [sem(f"rw_loaded{m}") for m in range(RING)]
        w_down_loaded = [sem(f"w_down_loaded{m}") for m in range(RING)]
        decay_ready = sem("decay_ready")
        b_ready = sem("b_ready")
        scanned = sem("scanned")
        turned = sem("turned")
        added = sem("added")
        pair_filled = sem("pair_filled")
        pair_tanh = sem("pair_tanh")
        pair_mul = sem("pair_mul")
        pair_ready = sem("pair_ready")
        pair_used = sem("pair_used")
        y_turned = sem("y_turned")
        y_step = sem("y_step")
        y_ready = sem("y_ready")
        out_filled = sem("out_filled")
        res_loaded = sem("res_loaded")
        res_ready = sem("res_ready")
        stored = sem("stored")

        def wait_alone(eng, signal, value):
            if not isinstance(value, int):
                eng.wait_ge(started, 1)
            eng.wait_ge(signal, value)

        splits = [(w_in[0][:, k, :], w_in[1][:, k, :], w_in_d[k * P:(k + 1) * P, :]) for k in range(HT)]
        es, us = X // WGROUPS, X // WGROUPS * U
        for g in range(WGROUPS):
            for dst, src in ((w_gate, w_gate_d), (w_up, w_up_d)):
                for k in range(HT):
                    splits.append((dst[0][:, k, g * us:(g + 1) * us], dst[1][:, k, g * us:(g + 1) * us],
                                   src[g * es:(g + 1) * es, k * P:(k + 1) * P, :].rearrange("e p i -> p e i")))

        def first_pair(i, p=0):
            return isinstance(i, int) and i == 0 and p == 0

        def filled(i, name):
            return i * NF + FRONT.index(name) + 1

        def read_a(i, name):
            return i * NA + FRONT.index(name) - NV + 1

        def blocks(eng, body):
            body(0, 0, True, False)
            with eng.Fori(0, (BLOCKS - 2) // 2) as g:
                body(2 * g + 1, 1, False, False)
                body(2 * g + 2, 0, False, False)
            body(BLOCKS - 1, 1, False, True)

        block = ctx.enter_context(nc.Block())

        @block.sync
        def _(sp):
            def tokens(dram, i):
                one = dram[i, :, :] if isinstance(i, int) else dram[bass.ds(i, 1), :, :].rearrange("o t h -> (o t) h")
                return one.rearrange("(c p) h -> p c h", p=P)

            def load_x(i):
                sp.dma_start(x_in[:, :, :], tokens(x_d, i)).then_inc(x_loaded, 16)

            def load_rw(q, p):
                for t, lo, hi, e in pieces(p):
                    sp.dma_start(rw_rep[lo:hi, p % RING, t, :], rw_dram[q, e:e + 1, :].broadcast_to([hi - lo, T])).then_inc(rw_loaded[p % RING], 16)

            def load_down(p, tiles=(0, 1)):
                for t in tiles:
                    rows = w_down_d.rearrange("e i h -> (e i) h")[(2 * p + t) * P:(2 * p + t + 1) * P, :]
                    sp.dma_start(w_down[:, p % RING, t, :], rows).then_inc(w_down_loaded[p % RING], 16)

            def load_b(q, c):
                src = b_dram[q, c * BCH:(c + 1) * BCH, :]
                sp.dma_start(b_rep[:, c % 2, :, :], src[None, :, :].broadcast_to([P, BCH, T])).then_inc(b_loaded[c % 2], 16)

            load_x(0)
            sp.dma_start(router_rows, router_d).then_inc(w_small_loaded, 16)
            sp.dma_start(neg_a[:, :, :], a_log_d.rearrange("(c p) n -> p c n", p=P)).then_inc(w_small_loaded, 16)
            sp.dma_start(conv_k[:, :, :], conv_k_d.rearrange("(c p) o k -> p c (o k)", p=P)).then_inc(w_small_loaded, 16)
            for dst, src in ((conv_b, conv_b_d), (b_dt, b_dt_d), (d_half, d_d)):
                sp.dma_start(dst[:, :], src.rearrange("(c p) -> p c", p=P), allow_slow_non_contiguous=True).then_inc(w_small_loaded, 16)
            for k, (hi, lo, src) in enumerate(splits):
                m = k % len(staging)
                if k >= len(staging):
                    sp.wait_ge(split, k - len(staging) + 1)
                dst = staging[m][:, 0:hi.shape[1]]
                if len(src.shape) == 3:
                    dst = dst.rearrange("p (e i) -> p e i", e=es)
                sp.dma_start(dst, src).then_inc(staged[m], 16)
                if k == 1:
                    sp.dma_start(w_x[:, :, :], w_x_d.rearrange("(k p) e -> p k e", p=P)).then_inc(w_front_loaded, 16)
                    sp.dma_start(w_dt[:, :], w_dt_d).then_inc(w_front_loaded, 16)
                if k == 6:
                    sp.wait_ge(rw_stored, 16)
                    for p in range(RING):
                        load_down(p)
                    for p in range(2):
                        load_rw(0, p)
                if k == 8:
                    sp.wait_ge(b_stored, 16)
                    for c in range(2):
                        load_b(0, c)
            sp.wait_ge(front_filled, 1)
            load_x(1)
            sp.dma_start(w_out[:, :, :], w_out_d.rearrange("(k p) h -> p k h", p=P)).then_inc(w_late_loaded, 16)

            def store(i):
                wait_alone(sp, res_ready, i + 1)
                sp.dma_start(tokens(out_d, i), res[:, :, :]).then_inc(stored, 16)

            def residual(i, first):
                if not first:
                    wait_alone(sp, stored, i * 16)
                sp.dma_start(res[:, :, :], tokens(x_d, i)).then_inc(res_loaded, 16)

            def main(i, q, first, last, ahead):
                for p in range(PAIRS):
                    if p + 2 < PAIRS or not last:
                        if not (first and p == 0):
                            sp.wait_ge(pair_ready, i * PAIRS + p)
                        load_rw(q if p + 2 < PAIRS else 1 - q, (p + 2) % PAIRS)
                    if p == 1 and ahead:
                        sp.wait_ge(front_filled, filled(i + 1, "xnT"))
                        load_x(i + 2)
                    if p == 3 and not first:
                        store(i - 1)
                    if p == 5:
                        residual(i, first)
                    if (p + 2 < PAIRS or not last) and not (first and p == 0):
                        sp.wait_ge(pair_used, i * PAIRS + p)
                        load_down((p + 2) % PAIRS, (0,))
                        if p == 9 and not last:
                            sp.wait_ge(rw_stored, (i + 2) * 16)
                        if p == 7 and not last:
                            sp.wait_ge(b_stored, (i + 2) * 16)
                        load_down((p + 2) % PAIRS, (1,))
                    for c in range(CHUNKS):
                        if p == [0, 1, 3, 4, 6, 7, 9, 11][c] and (c + 2 < CHUNKS or not last):
                            sp.wait_ge(b_ready, i * NS + (c + 1) * BCH)
                            load_b(q if c + 2 < CHUNKS else 1 - q, (c + 2) % CHUNKS)

            main(0, 0, True, False, True)
            with sp.Fori(0, (BLOCKS - 2) // 2 - 1) as g:
                main(2 * g + 1, 1, False, False, True)
                main(2 * g + 2, 0, False, False, True)
            main(BLOCKS - 3, 1, False, False, True)
            main(BLOCKS - 2, 0, False, False, False)
            main(BLOCKS - 1, 1, False, True, False)
            store(BLOCKS - 1)
            sp.wait_ge(stored, BLOCKS * 16)
            sp.wait_ge(rw_stored, BLOCKS * 16)
            sp.wait_ge(b_stored, BLOCKS * 16)

        @block.gpsimd
        def _(pool):
            pool.memset(minus_half[:, :], -0.5).then_inc(started, 1)
            pool.memset(eps[:, :], 1e-5).then_inc(started, 1)
            pool.memset(ident[:, :], 0.0).then_inc(zeroed, 1)
            pool.memset(hp[:, :, :, 0:PAD], 0.0).then_inc(zeroed, 1)
            pool.wait_ge(zeroed, 1)
            pool.affine_select(out=ident[:, :], in_=ident[:, :], compare_op=ALU.not_equal, fill=1.0, base=0,
                               pattern=[[-1, P]], channel_multiplier=1).then_inc(ident_ready, 1)

            def norm(i):
                pool.wait_ge(started, 2)
                pool.wait_ge(moments_ready, i + 1)
                pool.tensor_tensor(var_eps[:, :], moments[:, :, 1], eps[:, :], ALU.add).then_inc(var_ready, 1)
                pool.wait_ge(var_ready, i + 1)
                pool.tensor_tensor(rstd[:, :], var_eps[:, :], minus_half[:, :], ALU.pow).then_inc(rstd_ready, 1)

            def step_input(i, q):
                pool.wait_ge(dt_ready, i + 1)
                pool.tensor_tensor(du2[:, q, :, :], u2[:, q, :, :], dt[:, q, :, :], ALU.mult).then_inc(du_ready, 1)

            def state_input(i, q, n, m):
                if n == 0:
                    pool.wait_ge(du_ready, i + 1)
                if n % BCH == 0:
                    c = n // BCH
                    pool.wait_ge(b_loaded[c % 2], (i * (CHUNKS // 2) + c // 2 + 1) * 16)
                if not (isinstance(i, int) and i == 0 and n < 2):
                    pool.wait_ge(turned, i * NS + n - 1)
                pool.tensor_tensor(state[:, m, :, :], du2[:, q, :, :],
                                   b_rep[:, n // BCH % 2, n % BCH, :][:, None, :].broadcast_to([P, ET, T]), ALU.mult).then_inc(b_ready, 1)

            def weigh(i, p):
                pool.wait_ge(rw_loaded[p % RING], (i * (PAIRS // RING) + p // RING + 1) * 4 * 16)
                pool.wait_ge(pair_mul, i * PAIRS + p + 1)
                pool.tensor_tensor(moe[:, p % RING, :, :], moe[:, p % RING, :, :], rw_rep[:, p % RING, :, :], ALU.mult).then_inc(pair_ready, 1)

            norm(0)
            step_input(0, 0)
            pool.wait_ge(split, len(splits))
            pool.memset(decay[:, :, :, 0:1], 0.0).then_inc(zeroed, 1)
            state_input(0, 0, 0, 0)

            def main(i, q, first, last):
                for s in range(NS):
                    if s < NS - 1:
                        state_input(i, q, s + 1, (s + 1) % 2)
                    elif not last:
                        state_input(i + 1, 1 - q, 0, 0)
                    if s in PAIR_AT:
                        weigh(i, PAIR_AT.index(s))
                    if not last and s == 0:
                        norm(i + 1)
                    if not last and s == 14:
                        step_input(i + 1, 1 - q)

            blocks(pool, main)

        @block.scalar
        def _(act):
            act.wait_ge(w_small_loaded, 6 * 16)
            act.activation(neg_a[:, :, :], neg_a[:, :, :], ACT.Exp).then_inc(a_exp, 1)
            act.wait_ge(router_turned, 1)
            act.activation(router[0][:, :, :], front_ps[:, 0, 0:HT * X].rearrange("p (k e) -> p k e", k=HT), ACT.Copy).then_inc(router_hi, 1)

            def decays(i, q, n, m):
                if n == 0:
                    act.wait_ge(dt_ready, i + 1)
                if not (isinstance(i, int) and i == 0 and n < 2):
                    act.wait_ge(scanned, i * NS + n - 1)
                for e in range(ET):
                    last = act.activation(decay[:, m, e, 1:T], dt[:, q, e, 1:T], ACT.Exp, scale=neg_a[:, e, n:n + 1])
                last.then_inc(decay_ready, 1)

            def pair(i, p):
                act.wait_ge(pair_filled, i * PAIRS + p + 1)
                if not (isinstance(i, int) and i == 0 and p < RING):
                    act.wait_ge(pair_used, i * PAIRS + p - RING + 1)
                act.activation(moe[:, p % RING, :, :], pair_ps[:, p % 2, 0, :, :], ACT.Tanh, scale=0.5).then_inc(pair_tanh, 1)

            def front(name, i, q):
                act.wait_ge(front_filled, filled(i, name))
                if name == "xnT":
                    act.activation(xnT[0][:, q, :, :], front_ps[:, :, :], ACT.Copy).then_inc(xnT_hi, 1)
                elif name in ("hid0", "hid1"):
                    e = 2 * (name == "hid1")
                    if first_pair(i) and name == "hid0":
                        act.wait_ge(zeroed, 2)
                    act.activation(hp[:, q, e:e + 2, PAD:], front_ps[:, :, :], ACT.Copy).then_inc(front_read_a, 1)
                elif name == "weightsT":
                    act.activation(rwT, front_ps[0:X, 0, :], ACT.Copy).then_inc(front_read_a, 1)
                    act.wait_ge(front_read_a, read_a(i, name))
                    act.dma_start(rw_dram[q, :, :], rwT).then_inc(rw_stored, 16)
                elif name == "low":
                    act.wait_ge(rw_stored, (i + 1) * 16)
                    act.activation(low[:, :], front_ps[:, 0, :], ACT.Copy, scale=0.5)
                    if not first_pair(i):
                        act.wait_ge(b_stored, i * 16)
                    act.activation(bcT[:, :], front_ps[0:2 * NS, 1, :], ACT.Copy, scale=0.5).then_inc(front_read_a, 1)
                    act.wait_ge(front_read_a, read_a(i, name))
                    act.dma_start(b_dram[q, :, :], bcT[0:NS, :]).then_inc(b_stored, 16)
                elif name == "C":
                    act.activation(c_tok[:, q, :, :], front_ps[:, 0, 0:TT * 2 * NS].rearrange("p (t n) -> p t n", t=TT),
                                   ACT.Copy, scale=0.5).then_inc(front_read_a, 1)
                elif name in ("dt0", "dt1"):
                    e = 2 * (name == "dt1")
                    for j in range(2):
                        last = act.activation(conv[:, q, e + j, :], front_ps[:, j, :], ACT.Identity, bias=b_dt[:, e + j:e + j + 1])
                    last.then_inc(front_read_a, 1)

            def gate(i, half):
                act.wait_ge(gate_filled, 2 * i + half + 1)
                if half == 0 and not first_pair(i):
                    act.wait_ge(y_ready, 2 * i)
                act.activation(gate2[:, 2 * half:2 * half + 2, :], front_ps[:, :, :], ACT.Tanh, scale=0.5).then_inc(gate_tanh, 1)

            def router_exp(i):
                act.wait_ge(lmax_ready, i * 2 + 2)
                act.activation(expl[:, :, :], logit[:, :, :], ACT.Exp).then_inc(expl_ready, 1)

            def conv_first(i, q):
                act.wait_ge(front_read_a, read_a(i, "hid1"))
                for e in range(ET):
                    last = act.activation(conv[:, q, e, :], hp[:, q, e, 0:T], ACT.Identity, bias=conv_b[:, e:e + 1], scale=conv_k[:, e, 0:1])
                last.then_inc(z_ready, 1)

            def conv_silu(i, q):
                act.wait_ge(conv_step, i * 3 + 3)
                act.activation(tmp[:, q, :, :], conv[:, q, :, :], ACT.Tanh, scale=0.5).then_inc(conv_tanh, 1)

            def softplus(i, q):
                act.wait_ge(nabs_ready, i + 1)
                act.activation(tmp[:, q, :, :], tmp[:, q, :, :], ACT.Exp).then_inc(soft_step, 1)
                act.wait_ge(soft_step, 2 * i + 1)
                act.activation(tmp[:, q, :, :], tmp[:, q, :, :], ACT.Ln, bias=1.0).then_inc(soft_step, 1)

            def front_at(s, i, q):
                for name in FRONT:
                    if STEP[name] == s:
                        front(name, i, q)
                if s == 3:
                    router_exp(i)
                if s == 4:
                    conv_first(i, q)
                if s == 6:
                    conv_silu(i, q)
                if s == 13:
                    softplus(i, q)

            for s in range(NS):
                front_at(s, 0, 0)
            act.wait_ge(zeroed, 3)
            decays(0, 0, 0, 0)

            def main(i, q, first, last):
                for s in range(NS):
                    if s < NS - 1:
                        decays(i, q, s + 1, (s + 1) % 2)
                    elif not last:
                        decays(i + 1, 1 - q, 0, 0)
                    if s in PAIR_AT:
                        pair(i, PAIR_AT.index(s))
                    if not last:
                        front_at(s, i + 1, 1 - q)
                    if s in GATE_STEP:
                        gate(i, GATE_STEP.index(s))

            blocks(act, main)

        @block.vector
        def _(dve):
            def split_weights(k):
                hi, lo, _ = splits[k]
                m = k % len(staging)
                raw = staging[m][:, 0:hi.shape[1]]
                dve.wait_ge(staged[m], (k // len(staging) + 1) * 16)
                dve.tensor_copy(hi, raw).then_inc(split_hi, 1)
                dve.wait_ge(split_hi, k + 1)
                dve.tensor_tensor(lo, raw, hi.bitcast(F32), ALU.subtract).then_inc(split, 1)

            dve.wait_ge(router_hi, 1)
            dve.tensor_tensor(router[1][:, :, :], front_ps[:, 0, 0:HT * X].rearrange("p (k e) -> p k e", k=HT),
                              router[0][:, :, :].bitcast(F32), ALU.subtract).then_inc(router_ready, 1)
            dve.wait_ge(a_exp, 1)
            dve.tensor_scalar(neg_a[:, :, :], neg_a[:, :, :], -1.0, None, ALU.mult).then_inc(a_ready, 1)
            dve.tensor_scalar(d_half[:, :], d_half[:, :], 0.5, None, ALU.mult).then_inc(a_ready, 1)

            def norm(i):
                dve.wait_ge(x_loaded, (i + 1) * 16)
                for c in range(TT):
                    last = dve.bn_stats(stats[:, c, :], x_in[:, c, :])
                last.then_inc(stats_ready, 1)
                wait_alone(dve, stats_ready, i + 1)
                for c in range(TT):
                    last = dve.bn_aggr(moments[:, c, :], stats[:, c, :])
                last.then_inc(moments_ready, 1)

            def normed(i):
                dve.wait_ge(rstd_ready, i + 1)
                for c in range(TT):
                    last = dve.tensor_scalar(x_in[:, c, :], x_in[:, c, :], moments[:, c, 0:1], rstd[:, c:c + 1],
                                             ALU.subtract, ALU.mult)
                last.then_inc(xn_ready, 1)

            def turned_lo(i, q):
                dve.wait_ge(xnT_hi, i + 1)
                dve.tensor_tensor(xnT[1][:, q, :, :], front_ps[:, :, :], xnT[0][:, q, :, :].bitcast(F32), ALU.subtract).then_inc(front_read_v, 1)

            def logits(i):
                ps = front_ps[:, 0, 0:TT * X].rearrange("p (t e) -> p t e", t=TT)
                dve.wait_ge(front_filled, filled(i, "logits"))
                dve.tensor_reduce(lmax[:, :], ps, AX_X, ALU.max).then_inc(lmax_ready, 1)
                dve.wait_ge(lmax_ready, 2 * i + 1)
                dve.tensor_tensor(logit[:, :, :], ps, lmax[:, :, None].broadcast_to([P, TT, X]), ALU.subtract).then_inc(lmax_ready, 1)

            def route(i):
                wait_alone(dve, expl_ready, i + 1)
                for c in range(TT):
                    last = dve.max(top[:, c, :], expl[:, c, :])
                last.then_inc(top_ready, 1)
                wait_alone(dve, top_ready, i + 1)
                for c in range(TT):
                    dve.match_replace(rest[:, c, :], top[:, c, :], expl[:, c, :], -1.0)
                dve.tensor_reduce(topsum[:, :], top[:, :, :], AX_X, ALU.add).then_inc(rw_step, 1)
                dve.wait_ge(rw_step, 3 * i + 1)
                dve.reciprocal(inv[:, :], topsum[:, :]).then_inc(rw_step, 1)
                dve.scalar_tensor_tensor(out=rest[:, :, :], in0=rest[:, :, :], scalar=0.0, in1=expl[:, :, :],
                                         op0=ALU.is_lt, op1=ALU.mult).then_inc(rw_step, 1)
                dve.wait_ge(rw_step, 3 * i + 3)
                if not (isinstance(i, int) and i == 0):
                    dve.wait_ge(front_filled, filled(i - 1, "weightsT"))
                dve.scalar_tensor_tensor(out=rw[:, :, :], in0=rest[:, :, :], scalar=0.5,
                                         in1=inv[:, :, None].broadcast_to([P, TT, X]), op0=ALU.mult, op1=ALU.mult).then_inc(rw_ready, 1)

            def gate(i, half):
                dve.wait_ge(gate_tanh, 2 * i + half + 1)
                g = gate2[:, 2 * half:2 * half + 2, :]
                dve.scalar_tensor_tensor(out=g, in0=g, scalar=1.0, in1=front_ps[:, :, :], op0=ALU.add, op1=ALU.mult).then_inc(gate_read, 1)

            def taps(i, q):
                dve.wait_ge(z_ready, i + 1)
                for k in range(1, TAPS):
                    if k > 1:
                        dve.wait_ge(conv_step, 3 * i + k - 1)
                    for e in range(ET):
                        last = dve.scalar_tensor_tensor(out=conv[:, q, e, :], in0=hp[:, q, e, k:k + T], scalar=conv_k[:, e, k:k + 1],
                                                        in1=conv[:, q, e, :], op0=ALU.mult, op1=ALU.add)
                    last.then_inc(conv_step, 1)

            def silu(i, q):
                dve.wait_ge(conv_tanh, i + 1)
                dve.scalar_tensor_tensor(out=u2[:, q, :, :], in0=tmp[:, q, :, :], scalar=1.0, in1=conv[:, q, :, :],
                                         op0=ALU.add, op1=ALU.mult).then_inc(u2_ready, 1)

            def minus_abs(i, q):
                dve.wait_ge(front_read_a, (i + 1) * NA)
                dve.scalar_tensor_tensor(out=tmp[:, q, :, :], in0=conv[:, q, :, :], scalar=-1.0, in1=conv[:, q, :, :],
                                         op0=ALU.mult, op1=ALU.min).then_inc(nabs_ready, 1)

            def steps(i, q):
                dve.wait_ge(soft_step, 2 * i + 2)
                dve.scalar_tensor_tensor(out=dt[:, q, :, :], in0=conv[:, q, :, :], scalar=0.0, in1=tmp[:, q, :, :],
                                         op0=ALU.max, op1=ALU.add).then_inc(dt_ready, 1)

            def scan(i, n, m):
                dve.wait_ge(decay_ready, i * NS + n + 1)
                dve.wait_ge(b_ready, i * NS + n + 1)
                h = state[:, m, :, :].rearrange("p e t -> p (e t)")
                dve.tensor_tensor_scan(h, decay[:, m, :, :].rearrange("p e t -> p (e t)"), h, 0.0,
                                       ALU.mult, ALU.add).then_inc(scanned, 1)

            def add_state(i, q, n):
                for c in range(TT):
                    dve.wait_ge(turned, i * NS + n + 1)
                    scale = c_tok[:, q, c, NS + n:NS + n + 1]
                    if n == 0:
                        if not (isinstance(i, int) and i == 0):
                            dve.wait_ge(y_turned, i)
                        last = dve.tensor_scalar(acc[:, c, :], turn_ps[:, c, :], scale, None, ALU.mult)
                    else:
                        dve.wait_ge(added, i * NS + n)
                        last = dve.scalar_tensor_tensor(out=acc[:, c, :], in0=turn_ps[:, c, :], scalar=scale,
                                                        in1=acc[:, c, :], op0=ALU.mult, op1=ALU.add)
                last.then_inc(added, 1)

            def pair(i, p):
                dve.wait_ge(pair_tanh, i * PAIRS + p + 1)
                m = moe[:, p % RING, :, :]
                dve.scalar_tensor_tensor(out=m, in0=m, scalar=1.0, in1=pair_ps[:, p % 2, 0, :, :],
                                         op0=ALU.add, op1=ALU.mult).then_inc(y_step, 1)
                dve.wait_ge(y_step, i * PAIRS + p + 1)
                dve.tensor_tensor(m, m, pair_ps[:, p % 2, 1, :, :], ALU.mult).then_inc(pair_mul, 1)

            def gated(i, q):
                dve.wait_ge(y_turned, i + 1)
                for e in range(ET):
                    last = dve.scalar_tensor_tensor(out=u2[:, q, e, :], in0=u2[:, q, e, :], scalar=d_half[:, e:e + 1],
                                                    in1=turn_ps[:, e // 2, (e % 2) * T:(e % 2 + 1) * T], op0=ALU.mult, op1=ALU.add)
                last.then_inc(y_ready, 1)
                dve.wait_ge(y_ready, 2 * i + 1)
                dve.scalar_tensor_tensor(out=u2[:, q, :, :], in0=u2[:, q, :, :], scalar=0.5, in1=gate2[:, :, :],
                                         op0=ALU.mult, op1=ALU.mult).then_inc(y_ready, 1)

            def total(i):
                dve.wait_ge(out_filled, i + 1)
                dve.wait_ge(res_loaded, (i + 1) * 16)
                dve.tensor_tensor(res[:, :, :], res[:, :, :], out_ps[:, :, :], ALU.add).then_inc(res_ready, 1)

            def front_at(s, i, q):
                if s == 0:
                    norm(i)
                    normed(i)
                if s == 1:
                    turned_lo(i, q)
                if s == 2:
                    logits(i)
                if s == 3:
                    route(i)
                if s == 5:
                    taps(i, q)
                if s == 6:
                    silu(i, q)
                if s == 12:
                    minus_abs(i, q)
                if s == 13:
                    steps(i, q)

            for s in range(NS):
                front_at(s, 0, 0)
                for k in range(s * len(splits) // NS, (s + 1) * len(splits) // NS):
                    split_weights(k)

            def main(i, q, first, last):
                for s in range(NS):
                    scan(i, s, s % 2)
                    if s == 1 and not first:
                        gated(i - 1, 1 - q)
                    if s == 2 and not first:
                        total(i - 1)
                    if s > 0:
                        add_state(i, q, s - 1)
                    elif not first:
                        add_state(i - 1, 1 - q, NS - 1)
                    if s in PAIR_AT:
                        pair(i, PAIR_AT.index(s))
                    if not last:
                        front_at(s, i + 1, 1 - q)
                    if s in GATE_STEP:
                        gate(i, GATE_STEP.index(s))

            blocks(dve, main)
            end = BLOCKS - 1
            add_state(end, 1, NS - 1)
            gated(end, 1)
            total(end)

        @block.tensor
        def _(pe):
            pe.wait_ge(ident_ready, 1)
            pe.wait_ge(w_small_loaded, 6 * 16)
            for k in range(HT):
                last = pe.transpose(front_ps[:, 0, k * X:(k + 1) * X], router_rows[:, k * P:(k + 1) * P], ident[0:X, 0:X])
            last.then_inc(router_turned, 1)

            def split_product(out, w, x, start=True, stop=True):
                terms = [(k, a, b) for k in range(HT) for a, b in ((0, 0), (0, 1), (1, 0))]
                for at, (k, a, b) in enumerate(terms):
                    last = pe.matmul(out, w(a, k), x(b, k), start=(at == 0), stop=(at == len(terms) - 1))
                return last

            def front(name, i, q):
                if name == "xnT":
                    if first_pair(i):
                        pe.wait_ge(router_ready, 1)
                    elif not (isinstance(i, int) and i == 1):
                        pe.wait_ge(gate_read, 2 * (i - 1))
                    pe.wait_ge(xn_ready, i + 1)
                    for h in range(HT):
                        for c in range(TT):
                            last = pe.transpose(front_ps[:, h, c * P:(c + 1) * P], x_in[:, c, h * P:(h + 1) * P], ident[:, :])
                elif name == "logits":
                    pe.wait_ge(front_read_v, i + 1)
                    for c in range(TT):
                        last = split_product(front_ps[:, 0, c * X:(c + 1) * X], lambda a, k: xnT[a][:, q, k, c * P:(c + 1) * P],
                                             lambda b, k: router[b][:, k, :])
                elif name in ("hid0", "hid1"):
                    if name == "hid0":
                        pe.wait_ge(lmax_ready, 2 * i + 2)
                        if first_pair(i):
                            pe.wait_ge(split, HT)
                    else:
                        pe.wait_ge(front_read_a, read_a(i, "hid0"))
                    for j in range(2):
                        m = 2 * (name == "hid1") + j
                        last = split_product(front_ps[:, j, :], lambda a, k: w_in[a][:, k, m * P:(m + 1) * P],
                                             lambda b, k: xnT[b][:, q, k, :])
                elif name == "weightsT":
                    pe.wait_ge(front_read_a, read_a(i, "hid1"))
                    pe.wait_ge(rw_ready, i + 1)
                    for c in range(TT):
                        last = pe.transpose(front_ps[0:X, 0, c * P:(c + 1) * P], rw[:, c, :], ident[:, :])
                elif name == "low":
                    pe.wait_ge(front_read_a, read_a(i, "weightsT"))
                    if first_pair(i):
                        pe.wait_ge(w_front_loaded, 2 * 16)
                    pe.wait_ge(u2_ready, i + 1)
                    for e in range(ET):
                        last = pe.matmul(front_ps[:, 0, :], w_x[:, e, 0:R], u2[:, q, e, :], start=(e == 0), stop=(e == ET - 1))
                    for e in range(ET):
                        last = pe.matmul(front_ps[0:2 * NS, 1, :], w_x[:, e, R:R + 2 * NS], u2[:, q, e, :],
                                         start=(e == 0), stop=(e == ET - 1))
                elif name == "C":
                    pe.wait_ge(front_read_a, read_a(i, "low"))
                    for c in range(TT):
                        last = pe.matmul(front_ps[:, 0, c * 2 * NS:(c + 1) * 2 * NS], bcT[:, c * P:(c + 1) * P],
                                         ident[0:2 * NS, 0:2 * NS], start=True, stop=True)
                elif name in ("dt0", "dt1"):
                    pe.wait_ge(front_read_a, read_a(i, "C" if name == "dt0" else "dt0"))
                    for j in range(2):
                        m = 2 * (name == "dt1") + j
                        last = pe.matmul(front_ps[:, j, :], w_dt[:, m * P:(m + 1) * P], low[:, :], start=True, stop=True)
                last.then_inc(front_filled, 1)

            def gate(i, q, half, last):
                if half == 0:
                    if not last:
                        pe.wait_ge(front_read_a, read_a(i + 1, "dt1"))
                    else:
                        pe.wait_ge(gate_read, 2 * i)
                else:
                    pe.wait_ge(gate_read, 2 * i + 1)
                for j in range(2):
                    m = ET + 2 * half + j
                    done = split_product(front_ps[:, j, :], lambda a, k: w_in[a][:, k, m * P:(m + 1) * P],
                                         lambda b, k: xnT[b][:, q, k, :])
                done.then_inc(gate_filled, 1)

            def turn(i, n, m):
                pe.wait_ge(scanned, i * NS + n + 1)
                if n > 0:
                    pe.wait_ge(added, i * NS + n)
                elif not (isinstance(i, int) and i == 0):
                    pe.wait_ge(y_ready, 2 * i - 1)
                for c in range(TT):
                    for e in range(ET):
                        last = pe.transpose(turn_ps[:, c, e * P:(e + 1) * P], state[:, m, e, c * P:(c + 1) * P], ident[:, :])
                last.then_inc(turned, 1)

            def turn_y(i):
                pe.wait_ge(added, (i + 1) * NS)
                for e in range(ET):
                    for c in range(TT):
                        at = (e % 2) * T + c * P
                        last = pe.transpose(turn_ps[:, e // 2, at:at + P], acc[:, c, e * P:(e + 1) * P], ident[:, :])
                last.then_inc(y_turned, 1)

            def pair_in(i, q, p, which):
                if isinstance(i, int) and i == 0:
                    group = (2 * p + 1) * WGROUPS // UT
                    pe.wait_ge(split, HT + (group + 1) * 2 * HT)
                if which == 0 and not (isinstance(i, int) and i == 0 and p < 2):
                    pe.wait_ge(pair_mul, i * PAIRS + p - 1)
                for j in range(2):
                    t = 2 * p + j
                    last = split_product(pair_ps[:, p % 2, which, j, :], lambda a, k: (w_gate, w_up)[which][a][:, k, t * P:(t + 1) * P],
                                         lambda b, k: xnT[b][:, q, k, :])
                if which == 1:
                    last.then_inc(pair_filled, 1)

            def pair_out(i, p):
                pe.wait_ge(w_down_loaded[p % RING], (i * (PAIRS // RING) + p // RING + 1) * 2 * 16)
                pe.wait_ge(pair_ready, i * PAIRS + p + 1)
                if p == 0 and not first_pair(i):
                    pe.wait_ge(res_ready, i)
                for j in range(2):
                    for c in range(TT):
                        last = pe.matmul(out_ps[:, c, :], moe[:, p % RING, j, c * P:(c + 1) * P], w_down[:, p % RING, j, :],
                                         start=(p == 0 and j == 0 and c == 0), stop=False, skip_group_check=True)
                last.then_inc(pair_used, 1)

            def project_y(i, q):
                if isinstance(i, int) and i == 0:
                    pe.wait_ge(w_late_loaded, 16)
                pe.wait_ge(y_ready, 2 * i + 2)
                for e in range(ET):
                    for c in range(TT):
                        last = pe.matmul(out_ps[:, c, :], u2[:, q, e, c * P:(c + 1) * P], w_out[:, e, :],
                                         start=False, stop=(e == ET - 1), skip_group_check=True)
                last.then_inc(out_filled, 1)

            for name in FRONT:
                front(name, 0, 0)

            def main(i, q, first, last):
                for s in range(NS):
                    if s == 0 and not first:
                        turn(i - 1, NS - 1, 1)
                    if s == 1 and not first:
                        turn_y(i - 1)
                    for h in halves(s):
                        p, which = h // 2, h % 2
                        pair_in(i, q, p, which)
                        if which == 1 and p >= 2:
                            pair_out(i, p - 2)
                        elif which == 1 and not first:
                            pair_out(i - 1, PAIRS - 2 + p)
                    if s == 2 and not first:
                        project_y(i - 1, 1 - q)
                    if s > 0:
                        turn(i, s - 1, (s - 1) % 2)
                    for name in FRONT:
                        if not last and STEP[name] == s:
                            front(name, i + 1, 1 - q)
                    if s in GATE_STEP:
                        gate(i, q, GATE_STEP.index(s), last)

            blocks(pe, main)
            end = BLOCKS - 1
            turn(end, NS - 1, 1)
            pair_out(end, PAIRS - 2)
            pair_out(end, PAIRS - 1)
            turn_y(end)
            project_y(end, 1)


_INS = ['L0_attn_input_states', 'L0_attn_W_in', 'L0_attn_conv_kernel', 'L0_attn_conv_bias', 'L0_attn_W_x',
        'L0_attn_W_dt', 'L0_attn_b_dt', 'L0_attn_W_out', 'L0_attn_A_log', 'L0_attn_D', 'L0_ffn_router_w',
        'L0_ffn_w_gate', 'L0_ffn_w_up', 'L0_ffn_w_down']


def kernel(**inputs):
    import numpy as _np
    import concourse.bacc as _bacc
    from concourse import mybir as _mybir
    from concourse.bass_utils import run_bass_kernel_spmd as _run

    nc = _bacc.Bacc("TRN2", target_bir_lowering=False, num_devices=1)
    arrays, args = {}, []
    for name in _INS:
        a = _np.ascontiguousarray(inputs[name])
        arrays[f"in_{name}_dram"] = a
        args.append(nc.dram_tensor(f"in_{name}_dram", a.shape, _mybir.dt.from_np(a.dtype), kind="ExternalInput").ap())
    shape = inputs['L0_attn_input_states'].shape
    args.append(nc.dram_tensor("out_0_dram", shape, _mybir.dt.float32, kind="ExternalOutput").ap())
    build(nc, *args)
    r = _run(nc, [arrays], core_ids=[0])
    return r.results[0]["out_0_dram"]
```

```python
from contextlib import ExitStack

import concourse.bass as bass
from concourse import mybir

F32 = mybir.dt.float32
F32R = mybir.dt.float32r
ALU = mybir.AluOpType
ACT = mybir.ActivationFunctionType
AX_X = mybir.AxisListType.X
P = 128


def build(nc, x_d, w_in_d, conv_k_d, conv_b_d, w_x_d, w_dt_d, b_dt_d, w_out_d, a_log_d, d_d,
          router_d, w_gate_d, w_up_d, w_down_d, out_d):
    BLOCKS, T, H = x_d.shape
    E, NS = a_log_d.shape
    TAPS = conv_k_d.shape[2]
    R = w_dt_d.shape[0]
    X, _, U = w_gate_d.shape
    TT, HT, ET = T // P, H // P, E // P
    UT = X * U // P
    PAIRS = UT // 2
    TOPK = 8
    assert (TT, HT, ET, R, NS) == (2, 2, 4, P, 16) and BLOCKS % 2 == 0 and UT == 24

    HALVES = [2, 2, 1, 0, 2, 2, 2, 2, 2, 1, 1, 1, 2, 1, 1, 2]
    assert HALVES[0] == 2 and len(HALVES) == NS and sum(HALVES) == 2 * PAIRS

    def halves(s):
        return range(sum(HALVES[:s]), sum(HALVES[:s + 1]))

    PAIR_AT = [s for p in range(PAIRS) for s in range(NS) if 2 * p + 1 in halves(s)]
    FRONT = ["xnT", "hid0", "hid1", "logits", "weightsT", "low", "dt0", "dt1", "C"]
    STEP = {"xnT": 1, "hid0": 2, "hid1": 3, "logits": 4, "weightsT": 8, "low": 9, "dt0": 10, "dt1": 11, "C": 12}
    AHEAD_AFTER = ("logits", "C")
    TAP_STEP = (5, 6)
    GATE_STEP = (13, 14)
    BY_SCALAR = [name for name in FRONT if name not in ("xnT", "logits")]
    NF, NA = len(FRONT), len(BY_SCALAR)
    BCH = 2
    CHUNKS = NS // BCH
    RING = 3
    WGROUPS = 4

    def pieces(p):
        found = []
        for t in range(2):
            at = (2 * p + t) * P
            for e in range(at // U, (at + P - 1) // U + 1):
                found.append((t, max(e * U - at, 0), min((e + 1) * U - at, P), e))
        return found

    assert all(len(pieces(p)) == 4 for p in range(PAIRS)) and PAIRS % RING == 0

    with ExitStack() as ctx:
        def sb(name, shape, dtype=F32):
            return ctx.enter_context(nc.sbuf_tensor(name, shape, dtype))

        def pb(name, shape):
            return ctx.enter_context(nc.psum_tensor(name, shape, F32))

        def sem(name):
            return ctx.enter_context(nc.semaphore(name))

        w_gate = [sb(f"w_gate_{x}", [P, HT, UT * P], F32R) for x in ("hi", "lo")]
        w_up = [sb(f"w_up_{x}", [P, HT, UT * P], F32R) for x in ("hi", "lo")]
        w_in = [sb(f"w_in_{x}", [P, HT, 2 * E], F32R) for x in ("hi", "lo")]
        router = [sb(f"router_{x}", [P, HT, X], F32R) for x in ("hi", "lo")]
        w_x = sb("w_x", [P, ET, R + 2 * NS])
        w_dt = sb("w_dt", [P, E])
        w_out = sb("w_out", [P, ET, H])
        ident = sb("ident", [P, P])
        neg_a = sb("neg_a", [P, ET, NS])
        conv_k = sb("conv_k", [P, ET, TAPS])
        conv_b = sb("conv_b", [P, ET])
        b_dt = sb("b_dt", [P, ET])
        d_quarter = sb("d_quarter", [P, ET])
        x_in = sb("x_in", [P, TT, H])
        stats = sb("stats", [P, TT, 6])
        moments = sb("moments", [P, TT, 2])
        var_eps = sb("var_eps", [P, TT])
        minus_half = sb("minus_half", [P, TT])
        eps = sb("eps", [P, TT])
        rstd = sb("rstd", [P, TT])
        xnT = [sb(f"xnT_{x}", [P, 2, HT, T], F32R) for x in ("hi", "lo")]
        lmax = sb("lmax", [P, TT])
        logit = sb("logit", [P, TT, X])
        expl = sb("expl", [P, TT, X])
        top = sb("top", [P, TT, TOPK])
        rest = sb("rest", [P, TT, X])
        topsum = sb("topsum", [P, TT])
        inv = sb("inv", [P, TT])
        rw = logit
        low = sb("low", [P, T])
        rwT = low[0:X, :]
        bcT = sb("bcT", [2 * NS, T])
        c_tok = sb("c_tok", [P, 2, TT, 2 * NS])
        PAD = TAPS - 1
        u2p = sb("u2p", [P, 2, ET, PAD + T])
        hp = u2p
        u2 = u2p[:, :, :, PAD:]
        dt = sb("dt", [P, 2, ET, T])
        conv = dt
        du2 = sb("du2", [P, 2, ET, T])
        tmp = du2
        gate2 = sb("gate2", [P, ET, T])
        b_rep = sb("b_rep", [P, 2, BCH, T])
        rw_rep = sb("rw_rep", [P, RING, 2, T])
        w_down = sb("w_down", [P, RING, 2, H])
        decay = sb("decay", [P, 2, ET, T])
        state = sb("state", [P, 2, ET, T])
        acc = sb("acc", [P, TT, E])
        moe = sb("moe", [P, RING, 2, T])
        res = sb("res", [P, TT, H])
        staging = [x[:, m, :, :].rearrange("p e t -> p (e t)") for x in (decay, state) for m in range(2)]
        router_rows = acc[0:X, 0, 0:H]

        pair_ps = pb("pair_ps", [P, 2, 2, 2, T])
        turn_ps = pb("turn_ps", [P, TT, E])
        out_ps = pb("out_ps", [P, TT, H])
        front_ps = pb("front_ps", [P, 2, T])

        rw_dram = nc.dram_tensor("rw_dram", [2, X, T], F32).ap()
        b_dram = nc.dram_tensor("b_dram", [2, NS, T], F32).ap()

        w_small_loaded = sem("w_small_loaded")
        w_front_loaded = sem("w_front_loaded")
        w_late_loaded = sem("w_late_loaded")
        staged = [sem(f"staged{k}") for k in range(len(staging))]
        split_hi = sem("split_hi")
        split = [sem(f"split_by_{x}") for x in ("vector", "pool")]
        router_hi = sem("router_hi")
        zeroed = sem("zeroed")
        started = sem("started")
        ident_ready = sem("ident_ready")
        router_turned = sem("router_turned")
        router_ready = sem("router_ready")
        a_exp = sem("a_exp")
        a_ready = sem("a_ready")
        x_loaded = sem("x_loaded")
        stats_ready = sem("stats_ready")
        moments_ready = sem("moments_ready")
        var_ready = sem("var_ready")
        rstd_ready = sem("rstd_ready")
        xn_ready = sem("xn_ready")
        front_filled = sem("front_filled")
        front_read_a = sem("front_read_a")
        front_read_v = sem("front_read_v")
        lmax_ready = sem("lmax_ready")
        expl_ready = sem("expl_ready")
        top_ready = sem("top_ready")
        rw_step = sem("rw_step")
        rw_ready = sem("rw_ready")
        rw_stored = sem("rw_stored")
        b_stored = sem("b_stored")
        xnT_hi = sem("xnT_hi")
        gate_filled = sem("gate_filled")
        gate_tanh = sem("gate_tanh")
        gate_read = sem("gate_read")
        conv_step = sem("conv_step")
        conv_tanh = sem("conv_tanh")
        u2_ready = sem("u2_ready")
        z_ready = sem("z_ready")
        soft_step = sem("soft_step")
        dt_ready = sem("dt_ready")
        du_ready = sem("du_ready")
        b_loaded = [sem(f"b_loaded{c}") for c in range(2)]
        rw_loaded = [sem(f"rw_loaded{m}") for m in range(RING)]
        w_down_loaded = [sem(f"w_down_loaded{m}") for m in range(RING)]
        decay_ready = sem("decay_ready")
        b_ready = sem("b_ready")
        scanned = sem("scanned")
        turned = sem("turned")
        added = sem("added")
        pair_filled = sem("pair_filled")
        pair_tanh = sem("pair_tanh")
        pair_mul = sem("pair_mul")
        pair_ready = sem("pair_ready")
        pair_used = sem("pair_used")
        y_turned = sem("y_turned")
        y_step = sem("y_step")
        y_ready = sem("y_ready")
        out_filled = sem("out_filled")
        res_loaded = sem("res_loaded")
        res_ready = sem("res_ready")
        stored = sem("stored")

        def wait_alone(eng, signal, value):
            if not isinstance(value, int):
                eng.wait_ge(started, 1)
            eng.wait_ge(signal, value)

        splits = [(w_in[0][:, k, :], w_in[1][:, k, :], w_in_d[k * P:(k + 1) * P, :]) for k in range(HT)]
        es, us = X // WGROUPS, X // WGROUPS * U
        for g in range(WGROUPS):
            for dst, src in ((w_gate, w_gate_d), (w_up, w_up_d)):
                for k in range(HT):
                    splits.append((dst[0][:, k, g * us:(g + 1) * us], dst[1][:, k, g * us:(g + 1) * us],
                                   src[g * es:(g + 1) * es, k * P:(k + 1) * P, :].rearrange("e p i -> p e i")))

        PER_STEP = [2, 0, 2, 0, 2, 0, 2, 2, 2, 2, 0, 2, 2, 0, 0, 0]
        SPLIT_AT = [range(sum(PER_STEP[:s]), sum(PER_STEP[:s + 1])) for s in range(NS)]
        assert sum(PER_STEP) == len(splits)

        def staged_part(k):
            return staging[k % len(staging)][:, 0:splits[k][0].shape[1]]

        def split_lo(eng, k):
            hi, lo, _ = splits[k]
            eng.wait_ge(split_hi, k + 1)
            eng.tensor_tensor(lo, staged_part(k), hi.bitcast(F32), ALU.subtract).then_inc(split[k % 2], 1)

        def wait_split(eng, count):
            for by in split:
                eng.wait_ge(by, count // 2)

        def first_pair(i, p=0):
            return isinstance(i, int) and i == 0 and p == 0

        def filled(i, name):
            return i * NF + FRONT.index(name) + 1

        def read_a(i, name):
            return i * NA + BY_SCALAR.index(name) + 1

        def blocks(eng, body):
            body(0, 0, True, False)
            with eng.Fori(0, (BLOCKS - 2) // 2) as g:
                body(2 * g + 1, 1, False, False)
                body(2 * g + 2, 0, False, False)
            body(BLOCKS - 1, 1, False, True)

        block = ctx.enter_context(nc.Block())

        @block.sync
        def _(sp):
            def tokens(dram, i):
                one = dram[i, :, :] if isinstance(i, int) else dram[bass.ds(i, 1), :, :].rearrange("o t h -> (o t) h")
                return one.rearrange("(c p) h -> p c h", p=P)

            def load_x(i):
                sp.dma_start(x_in[:, :, :], tokens(x_d, i)).then_inc(x_loaded, 16)

            def load_rw(q, p):
                for t, lo, hi, e in pieces(p):
                    sp.dma_start(rw_rep[lo:hi, p % RING, t, :], rw_dram[q, e:e + 1, :].broadcast_to([hi - lo, T])).then_inc(rw_loaded[p % RING], 16)

            def load_down(p, tiles=(0, 1)):
                for t in tiles:
                    rows = w_down_d.rearrange("e i h -> (e i) h")[(2 * p + t) * P:(2 * p + t + 1) * P, :]
                    sp.dma_start(w_down[:, p % RING, t, :], rows).then_inc(w_down_loaded[p % RING], 16)

            load_x(0)
            sp.dma_start(router_rows, router_d).then_inc(w_small_loaded, 16)
            sp.dma_start(neg_a[:, :, :], a_log_d.rearrange("(c p) n -> p c n", p=P)).then_inc(w_small_loaded, 16)
            sp.dma_start(conv_k[:, :, :], conv_k_d.rearrange("(c p) o k -> p c (o k)", p=P)).then_inc(w_small_loaded, 16)
            for dst, src in ((conv_b, conv_b_d), (b_dt, b_dt_d), (d_quarter, d_d)):
                sp.dma_start(dst[:, :], src.rearrange("(c p) -> p c", p=P), allow_slow_non_contiguous=True).then_inc(w_small_loaded, 16)
            for k, (hi, lo, src) in enumerate(splits):
                m = k % len(staging)
                if k >= len(staging):
                    sp.wait_ge(split[k % 2], (k - len(staging)) // 2 + 1)
                dst = staged_part(k)
                if len(src.shape) == 3:
                    dst = dst.rearrange("p (e i) -> p e i", e=es)
                sp.dma_start(dst, src).then_inc(staged[m], 16)
                if k == 1:
                    sp.dma_start(w_x[:, :, :], w_x_d.rearrange("(k p) e -> p k e", p=P)).then_inc(w_front_loaded, 16)
                    sp.dma_start(w_dt[:, :], w_dt_d).then_inc(w_front_loaded, 16)
            sp.wait_ge(rw_stored, 16)
            for p in range(2):
                load_rw(0, p)
            for p in range(RING):
                load_down(p)
            sp.wait_ge(front_filled, 1)
            load_x(1)
            sp.dma_start(w_out[:, :, :], w_out_d.rearrange("(k p) h -> p k h", p=P)).then_inc(w_late_loaded, 16)

            def store(i):
                wait_alone(sp, res_ready, i + 1)
                sp.dma_start(tokens(out_d, i), res[:, :, :]).then_inc(stored, 16)

            def residual(i, first):
                if not first:
                    wait_alone(sp, stored, i * 16)
                sp.dma_start(res[:, :, :], tokens(x_d, i)).then_inc(res_loaded, 16)

            def main(i, q, first, last, ahead):
                for p in range(PAIRS):
                    if p + 2 < PAIRS or not last:
                        if not (first and p == 0):
                            sp.wait_ge(pair_ready, i * PAIRS + p)
                        load_rw(q if p + 2 < PAIRS else 1 - q, (p + 2) % PAIRS)
                    if p == 1 and ahead:
                        sp.wait_ge(front_filled, filled(i + 1, "xnT"))
                        load_x(i + 2)
                    if p == 3 and not first:
                        store(i - 1)
                    if p == 5:
                        residual(i, first)
                    if (p + 2 < PAIRS or not last) and not (first and p == 0):
                        sp.wait_ge(pair_used, i * PAIRS + p)
                        load_down((p + 2) % PAIRS, (0,))
                        if p == 9 and not last:
                            sp.wait_ge(rw_stored, (i + 2) * 16)
                        load_down((p + 2) % PAIRS, (1,))

            main(0, 0, True, False, True)
            with sp.Fori(0, (BLOCKS - 2) // 2 - 1) as g:
                main(2 * g + 1, 1, False, False, True)
                main(2 * g + 2, 0, False, False, True)
            main(BLOCKS - 3, 1, False, False, True)
            main(BLOCKS - 2, 0, False, False, False)
            main(BLOCKS - 1, 1, False, True, False)
            store(BLOCKS - 1)
            sp.wait_ge(stored, BLOCKS * 16)
            sp.wait_ge(rw_stored, BLOCKS * 16)
            sp.wait_ge(b_stored, BLOCKS * 16)

        @block.gpsimd
        def _(pool):
            pool.memset(minus_half[:, :], -0.5).then_inc(started, 1)
            pool.memset(eps[:, :], 1e-5).then_inc(started, 1)
            pool.memset(ident[:, :], 0.0).then_inc(zeroed, 1)
            pool.memset(hp[:, :, :, 0:PAD], 0.0).then_inc(zeroed, 1)
            pool.wait_ge(zeroed, 1)
            pool.affine_select(out=ident[:, :], in_=ident[:, :], compare_op=ALU.not_equal, fill=1.0, base=0,
                               pattern=[[-1, P]], channel_multiplier=1).then_inc(ident_ready, 1)

            def norm(i):
                pool.wait_ge(started, 2)
                pool.wait_ge(moments_ready, i + 1)
                pool.tensor_tensor(var_eps[:, :], moments[:, :, 1], eps[:, :], ALU.add).then_inc(var_ready, 1)
                pool.wait_ge(var_ready, i + 1)
                pool.tensor_tensor(rstd[:, :], var_eps[:, :], minus_half[:, :], ALU.pow).then_inc(rstd_ready, 1)

            def step_input(i, q):
                pool.wait_ge(dt_ready, i + 1)
                pool.tensor_tensor(du2[:, q, :, :], u2[:, q, :, :], dt[:, q, :, :], ALU.mult).then_inc(du_ready, 1)

            def state_input(i, q, n, m):
                if n == 0:
                    pool.wait_ge(du_ready, i + 1)
                if n % BCH == 0:
                    c = n // BCH
                    pool.wait_ge(b_loaded[c % 2], (i * (CHUNKS // 2) + c // 2 + 1) * 16)
                if not (isinstance(i, int) and i == 0 and n < 2):
                    pool.wait_ge(turned, i * NS + n - 1)
                pool.tensor_tensor(state[:, m, :, :], du2[:, q, :, :],
                                   b_rep[:, n // BCH % 2, n % BCH, :][:, None, :].broadcast_to([P, ET, T]), ALU.mult).then_inc(b_ready, 1)

            def weigh(i, p):
                pool.wait_ge(rw_loaded[p % RING], (i * (PAIRS // RING) + p // RING + 1) * 4 * 16)
                pool.wait_ge(pair_mul, i * PAIRS + p + 1)
                pool.tensor_tensor(moe[:, p % RING, :, :], moe[:, p % RING, :, :], rw_rep[:, p % RING, :, :], ALU.mult).then_inc(pair_ready, 1)

            def tap_1(i, q):
                pool.wait_ge(z_ready, i + 1)
                pool.tensor_tensor(conv[:, q, :, :], conv[:, q, :, :], tmp[:, q, :, :], ALU.add).then_inc(conv_step, 1)

            def gated(i, q):
                pool.wait_ge(y_ready, 2 * i + 1)
                pool.tensor_tensor(u2[:, q, :, :], u2[:, q, :, :], gate2[:, :, :], ALU.mult).then_inc(y_ready, 1)

            norm(0)
            for k in range(1, len(splits), 2):
                split_lo(pool, k)
                if k == 3:
                    tap_1(0, 0)
            step_input(0, 0)
            wait_split(pool, len(splits))
            pool.memset(decay[:, :, :, 0:1], 0.0).then_inc(zeroed, 1)
            state_input(0, 0, 0, 0)

            def main(i, q, first, last):
                for s in range(NS):
                    if s == 1:
                        weigh(i, 0)
                        if not first:
                            gated(i - 1, 1 - q)
                    if s < NS - 1:
                        state_input(i, q, s + 1, (s + 1) % 2)
                    elif not last:
                        state_input(i + 1, 1 - q, 0, 0)
                    if not last and s == 0:
                        norm(i + 1)
                    if s > 1 and s - 1 in PAIR_AT:
                        weigh(i, PAIR_AT.index(s - 1))
                    elif s == 0 and not first:
                        weigh(i - 1, PAIRS - 1)
                    if not last and s == 4:
                        tap_1(i + 1, 1 - q)
                    if not last and s == 14:
                        step_input(i + 1, 1 - q)

            blocks(pool, main)
            weigh(BLOCKS - 1, PAIRS - 1)
            gated(BLOCKS - 1, 1)

        @block.scalar
        def _(act):
            act.wait_ge(w_small_loaded, 6 * 16)
            act.activation(neg_a[:, :, :], neg_a[:, :, :], ACT.Exp).then_inc(a_exp, 1)
            act.wait_ge(router_turned, 1)
            act.activation(router[0][:, :, :], front_ps[:, 0, 0:HT * X].rearrange("p (k e) -> p k e", k=HT), ACT.Copy).then_inc(router_hi, 1)

            def load_b(q, c):
                src = b_dram[q, c * BCH:(c + 1) * BCH, :]
                act.dma_start(b_rep[:, c % 2, :, :], src[None, :, :].broadcast_to([P, BCH, T])).then_inc(b_loaded[c % 2], 16)

            def decays(i, q, n, m):
                if n == 0:
                    act.wait_ge(dt_ready, i + 1)
                if not (isinstance(i, int) and i == 0 and n < 2):
                    act.wait_ge(scanned, i * NS + n - 1)
                for e in range(ET):
                    last = act.activation(decay[:, m, e, 1:T], dt[:, q, e, 1:T], ACT.Exp, scale=neg_a[:, e, n:n + 1])
                last.then_inc(decay_ready, 1)

            def pair(i, p):
                act.wait_ge(pair_filled, i * PAIRS + p + 1)
                if not (isinstance(i, int) and i == 0 and p < RING):
                    act.wait_ge(pair_used, i * PAIRS + p - RING + 1)
                act.activation(moe[:, p % RING, :, :], pair_ps[:, p % 2, 0, :, :], ACT.Tanh, scale=0.5).then_inc(pair_tanh, 1)

            def front(name, i, q):
                act.wait_ge(front_filled, filled(i, name))
                if name == "xnT":
                    act.activation(xnT[0][:, q, :, :], front_ps[:, :, :], ACT.Copy).then_inc(xnT_hi, 1)
                elif name in ("hid0", "hid1"):
                    e = 2 * (name == "hid1")
                    if first_pair(i) and name == "hid0":
                        act.wait_ge(zeroed, 2)
                    act.activation(hp[:, q, e:e + 2, PAD:], front_ps[:, :, :], ACT.Copy).then_inc(front_read_a, 1)
                elif name == "weightsT":
                    act.activation(rwT, front_ps[0:X, 0, :], ACT.Copy).then_inc(front_read_a, 1)
                    act.wait_ge(front_read_a, read_a(i, name))
                    act.dma_start(rw_dram[q, :, :], rwT).then_inc(rw_stored, 16)
                elif name == "low":
                    act.wait_ge(rw_stored, (i + 1) * 16)
                    act.activation(low[:, :], front_ps[:, 0, :], ACT.Copy, scale=0.5)
                    if not first_pair(i):
                        act.wait_ge(b_stored, i * 16)
                    act.activation(bcT[:, :], front_ps[0:2 * NS, 1, :], ACT.Copy, scale=0.5).then_inc(front_read_a, 1)
                    act.wait_ge(front_read_a, read_a(i, name))
                    act.dma_start(b_dram[q, :, :], bcT[0:NS, :]).then_inc(b_stored, 16)
                elif name == "C":
                    act.activation(c_tok[:, q, :, :], front_ps[:, 0, 0:TT * 2 * NS].rearrange("p (t n) -> p t n", t=TT),
                                   ACT.Copy, scale=0.25).then_inc(front_read_a, 1)
                elif name in ("dt0", "dt1"):
                    e = 2 * (name == "dt1")
                    for j in range(2):
                        last = act.activation(conv[:, q, e + j, :], front_ps[:, j, :], ACT.Identity, bias=b_dt[:, e + j:e + j + 1])
                    last.then_inc(front_read_a, 1)

            def gate(i, half):
                act.wait_ge(gate_filled, 2 * i + half + 1)
                if half == 0 and not first_pair(i):
                    act.wait_ge(y_ready, 2 * i)
                act.activation(gate2[:, 2 * half:2 * half + 2, :], front_ps[:, :, :], ACT.Tanh, scale=0.5).then_inc(gate_tanh, 1)

            def router_exp(i):
                act.wait_ge(lmax_ready, i * 2 + 2)
                act.activation(expl[:, :, :], logit[:, :, :], ACT.Exp).then_inc(expl_ready, 1)

            def conv_first(i, q):
                act.wait_ge(front_read_a, read_a(i, "hid1"))
                for e in range(ET):
                    act.activation(tmp[:, q, e, :], hp[:, q, e, 1:1 + T], ACT.Copy, scale=conv_k[:, e, 1:2])
                for e in range(ET):
                    last = act.activation(conv[:, q, e, :], hp[:, q, e, 0:T], ACT.Identity, bias=conv_b[:, e:e + 1], scale=conv_k[:, e, 0:1])
                last.then_inc(z_ready, 1)

            def conv_silu(i, q):
                act.wait_ge(conv_step, i * 3 + 3)
                act.activation(tmp[:, q, :, :], conv[:, q, :, :], ACT.Tanh, scale=0.5).then_inc(conv_tanh, 1)

            def minus_abs_exp(i, q):
                act.wait_ge(front_read_a, read_a(i, "dt1"))
                act.activation(tmp[:, q, :, :], conv[:, q, :, :], ACT.Abs).then_inc(soft_step, 1)
                act.wait_ge(soft_step, 3 * i + 1)
                act.activation(tmp[:, q, :, :], tmp[:, q, :, :], ACT.Exp, scale=-1.0).then_inc(soft_step, 1)

            def softplus(i, q):
                act.wait_ge(soft_step, 3 * i + 2)
                act.activation(tmp[:, q, :, :], tmp[:, q, :, :], ACT.Ln, bias=1.0).then_inc(soft_step, 1)

            def first_state(i, q):
                if not (isinstance(i, int) and i == 0):
                    act.wait_ge(y_turned, i)
                for c in range(TT):
                    act.wait_ge(turned, i * NS + 1)
                    last = act.activation(acc[:, c, :], turn_ps[:, c, :], ACT.Copy, scale=c_tok[:, q, c, NS:NS + 1])
                last.then_inc(added, 1)

            def front_at(s, i, q):
                if s == 12:
                    softplus(i, q)
                for name in FRONT:
                    if STEP[name] == s:
                        front(name, i, q)
                if s == 3:
                    conv_first(i, q)
                if s == 6:
                    router_exp(i)
                if s == 7:
                    conv_silu(i, q)
                if s == 11:
                    minus_abs_exp(i, q)

            for s in range(NS):
                front_at(s, 0, 0)
                for k in SPLIT_AT[s]:
                    act.wait_ge(staged[k % len(staging)], (k // len(staging) + 1) * 16)
                    act.activation(splits[k][0], staged_part(k), ACT.Copy).then_inc(split_hi, 1)
            act.wait_ge(b_stored, 16)
            for c in range(2):
                load_b(0, c)
            act.wait_ge(zeroed, 3)
            decays(0, 0, 0, 0)

            def main(i, q, first, last):
                for s in range(NS):
                    if s < NS - 1:
                        decays(i, q, s + 1, (s + 1) % 2)
                    elif not last:
                        decays(i + 1, 1 - q, 0, 0)
                    if s in PAIR_AT:
                        pair(i, PAIR_AT.index(s))
                    if s == 1:
                        first_state(i, q)
                    if not last:
                        front_at(s, i + 1, 1 - q)
                    if s in GATE_STEP:
                        gate(i, GATE_STEP.index(s))
                    c = (s - 1) // BCH
                    if s % BCH == 1 and (c + 2 < CHUNKS or not last):
                        if c + 2 == CHUNKS:
                            wait_alone(act, b_stored, (i + 2) * 16)
                        act.wait_ge(b_ready, i * NS + (c + 1) * BCH)
                        load_b(q if c + 2 < CHUNKS else 1 - q, (c + 2) % CHUNKS)

            blocks(act, main)

        @block.vector
        def _(dve):
            dve.wait_ge(router_hi, 1)
            dve.tensor_tensor(router[1][:, :, :], front_ps[:, 0, 0:HT * X].rearrange("p (k e) -> p k e", k=HT),
                              router[0][:, :, :].bitcast(F32), ALU.subtract).then_inc(router_ready, 1)
            dve.wait_ge(a_exp, 1)
            dve.tensor_scalar(neg_a[:, :, :], neg_a[:, :, :], -1.0, None, ALU.mult).then_inc(a_ready, 1)
            dve.tensor_scalar(d_quarter[:, :], d_quarter[:, :], 0.25, None, ALU.mult).then_inc(a_ready, 1)

            def norm(i):
                dve.wait_ge(x_loaded, (i + 1) * 16)
                for c in range(TT):
                    last = dve.bn_stats(stats[:, c, :], x_in[:, c, :])
                last.then_inc(stats_ready, 1)
                wait_alone(dve, stats_ready, i + 1)
                for c in range(TT):
                    last = dve.bn_aggr(moments[:, c, :], stats[:, c, :])
                last.then_inc(moments_ready, 1)

            def normed(i):
                dve.wait_ge(rstd_ready, i + 1)
                for c in range(TT):
                    last = dve.tensor_scalar(x_in[:, c, :], x_in[:, c, :], moments[:, c, 0:1], rstd[:, c:c + 1],
                                             ALU.subtract, ALU.mult)
                last.then_inc(xn_ready, 1)

            def turned_lo(i, q):
                dve.wait_ge(xnT_hi, i + 1)
                dve.tensor_tensor(xnT[1][:, q, :, :], front_ps[:, :, :], xnT[0][:, q, :, :].bitcast(F32), ALU.subtract).then_inc(front_read_v, 1)

            def logits(i):
                ps = front_ps[:, 0, 0:TT * X].rearrange("p (t e) -> p t e", t=TT)
                dve.wait_ge(front_filled, filled(i, "logits"))
                dve.tensor_reduce(lmax[:, :], ps, AX_X, ALU.max).then_inc(lmax_ready, 1)
                dve.wait_ge(lmax_ready, 2 * i + 1)
                dve.tensor_tensor(logit[:, :, :], ps, lmax[:, :, None].broadcast_to([P, TT, X]), ALU.subtract).then_inc(lmax_ready, 1)

            def route(i):
                wait_alone(dve, expl_ready, i + 1)
                for c in range(TT):
                    last = dve.max(top[:, c, :], expl[:, c, :])
                last.then_inc(top_ready, 1)
                wait_alone(dve, top_ready, i + 1)
                for c in range(TT):
                    dve.match_replace(rest[:, c, :], top[:, c, :], expl[:, c, :], -1.0)
                dve.tensor_reduce(topsum[:, :], top[:, :, :], AX_X, ALU.add).then_inc(rw_step, 1)
                dve.wait_ge(rw_step, 3 * i + 1)
                dve.reciprocal(inv[:, :], topsum[:, :]).then_inc(rw_step, 1)
                dve.scalar_tensor_tensor(out=rest[:, :, :], in0=rest[:, :, :], scalar=0.0, in1=expl[:, :, :],
                                         op0=ALU.is_lt, op1=ALU.mult).then_inc(rw_step, 1)
                dve.wait_ge(rw_step, 3 * i + 3)
                if not (isinstance(i, int) and i == 0):
                    dve.wait_ge(front_filled, filled(i - 1, "weightsT"))
                dve.scalar_tensor_tensor(out=rw[:, :, :], in0=rest[:, :, :], scalar=0.5,
                                         in1=inv[:, :, None].broadcast_to([P, TT, X]), op0=ALU.mult, op1=ALU.mult).then_inc(rw_ready, 1)

            def gate(i, half):
                dve.wait_ge(gate_tanh, 2 * i + half + 1)
                g = gate2[:, 2 * half:2 * half + 2, :]
                dve.scalar_tensor_tensor(out=g, in0=g, scalar=1.0, in1=front_ps[:, :, :], op0=ALU.add, op1=ALU.mult).then_inc(gate_read, 1)

            def taps(i, q, k):
                dve.wait_ge(conv_step, 3 * i + k - 1)
                for e in range(ET):
                    last = dve.scalar_tensor_tensor(out=conv[:, q, e, :], in0=hp[:, q, e, k:k + T], scalar=conv_k[:, e, k:k + 1],
                                                    in1=conv[:, q, e, :], op0=ALU.mult, op1=ALU.add)
                last.then_inc(conv_step, 1)

            def silu(i, q):
                dve.wait_ge(conv_tanh, i + 1)
                dve.scalar_tensor_tensor(out=u2[:, q, :, :], in0=tmp[:, q, :, :], scalar=1.0, in1=conv[:, q, :, :],
                                         op0=ALU.add, op1=ALU.mult).then_inc(u2_ready, 1)

            def steps(i, q):
                dve.wait_ge(soft_step, 3 * i + 3)
                dve.scalar_tensor_tensor(out=dt[:, q, :, :], in0=conv[:, q, :, :], scalar=0.0, in1=tmp[:, q, :, :],
                                         op0=ALU.max, op1=ALU.add).then_inc(dt_ready, 1)

            def scan(i, n, m):
                dve.wait_ge(decay_ready, i * NS + n + 1)
                dve.wait_ge(b_ready, i * NS + n + 1)
                h = state[:, m, :, :].rearrange("p e t -> p (e t)")
                dve.tensor_tensor_scan(h, decay[:, m, :, :].rearrange("p e t -> p (e t)"), h, 0.0,
                                       ALU.mult, ALU.add).then_inc(scanned, 1)

            def add_state(i, q, n):
                for c in range(TT):
                    dve.wait_ge(turned, i * NS + n + 1)
                    scale = c_tok[:, q, c, NS + n:NS + n + 1]
                    dve.wait_ge(added, i * NS + n)
                    last = dve.scalar_tensor_tensor(out=acc[:, c, :], in0=turn_ps[:, c, :], scalar=scale,
                                                    in1=acc[:, c, :], op0=ALU.mult, op1=ALU.add)
                last.then_inc(added, 1)

            def pair(i, p):
                dve.wait_ge(pair_tanh, i * PAIRS + p + 1)
                m = moe[:, p % RING, :, :]
                dve.scalar_tensor_tensor(out=m, in0=m, scalar=1.0, in1=pair_ps[:, p % 2, 0, :, :],
                                         op0=ALU.add, op1=ALU.mult).then_inc(y_step, 1)
                dve.wait_ge(y_step, i * PAIRS + p + 1)
                dve.tensor_tensor(m, m, pair_ps[:, p % 2, 1, :, :], ALU.mult).then_inc(pair_mul, 1)

            def gated_sum(i, q):
                dve.wait_ge(y_turned, i + 1)
                for e in range(ET):
                    last = dve.scalar_tensor_tensor(out=u2[:, q, e, :], in0=u2[:, q, e, :], scalar=d_quarter[:, e:e + 1],
                                                    in1=turn_ps[:, e // 2, (e % 2) * T:(e % 2 + 1) * T], op0=ALU.mult, op1=ALU.add)
                last.then_inc(y_ready, 1)

            def total(i):
                dve.wait_ge(out_filled, i + 1)
                dve.wait_ge(res_loaded, (i + 1) * 16)
                dve.tensor_tensor(res[:, :, :], res[:, :, :], out_ps[:, :, :], ALU.add).then_inc(res_ready, 1)

            def front_at(s, i, q):
                if s == 0:
                    normed(i)
                if s == 1:
                    turned_lo(i, q)
                if s == 5:
                    logits(i)
                if s == 7:
                    route(i)
                if s in TAP_STEP:
                    taps(i, q, 2 + TAP_STEP.index(s))
                if s == 8:
                    silu(i, q)
                if s == 13:
                    steps(i, q)

            norm(0)
            for s in range(NS):
                front_at(s, 0, 0)
                for k in SPLIT_AT[s][0::2]:
                    split_lo(dve, k)

            def main(i, q, first, last):
                for s in range(NS):
                    if s - 1 in GATE_STEP:
                        gate(i, GATE_STEP.index(s - 1))
                    if s == 1:
                        pair(i, 0)
                        if not first:
                            gated_sum(i - 1, 1 - q)
                    scan(i, s, s % 2)
                    if s == 0 and not last:
                        norm(i + 1)
                    if s > 1:
                        add_state(i, q, s - 1)
                    elif s == 0 and not first:
                        add_state(i - 1, 1 - q, NS - 1)
                    if s > 1 and s - 1 in PAIR_AT:
                        pair(i, PAIR_AT.index(s - 1))
                    elif s == 0 and not first:
                        pair(i - 1, PAIRS - 1)
                    if not last:
                        front_at(s, i + 1, 1 - q)
                    if s == 2 and not first:
                        total(i - 1)

            blocks(dve, main)
            end = BLOCKS - 1
            pair(end, PAIRS - 1)
            add_state(end, 1, NS - 1)
            gated_sum(end, 1)
            total(end)

        @block.tensor
        def _(pe):
            pe.wait_ge(ident_ready, 1)
            pe.wait_ge(w_small_loaded, 6 * 16)
            for k in range(HT):
                last = pe.transpose(front_ps[:, 0, k * X:(k + 1) * X], router_rows[:, k * P:(k + 1) * P], ident[0:X, 0:X])
            last.then_inc(router_turned, 1)

            def split_product(out, w, x, start=True, stop=True):
                terms = [(k, a, b) for k in range(HT) for a, b in ((0, 0), (0, 1), (1, 0))]
                for at, (k, a, b) in enumerate(terms):
                    last = pe.matmul(out, w(a, k), x(b, k), start=(at == 0), stop=(at == len(terms) - 1))
                return last

            def front(name, i, q):
                if name == "xnT":
                    if first_pair(i):
                        pe.wait_ge(router_ready, 1)
                    elif not (isinstance(i, int) and i == 1):
                        pe.wait_ge(gate_read, 2 * (i - 1))
                    pe.wait_ge(xn_ready, i + 1)
                    for h in range(HT):
                        for c in range(TT):
                            last = pe.transpose(front_ps[:, h, c * P:(c + 1) * P], x_in[:, c, h * P:(h + 1) * P], ident[:, :])
                elif name == "logits":
                    pe.wait_ge(front_read_a, read_a(i, "hid1"))
                    for c in range(TT):
                        last = split_product(front_ps[:, 0, c * X:(c + 1) * X], lambda a, k: xnT[a][:, q, k, c * P:(c + 1) * P],
                                             lambda b, k: router[b][:, k, :])
                elif name in ("hid0", "hid1"):
                    if name == "hid0":
                        pe.wait_ge(front_read_v, i + 1)
                        if first_pair(i):
                            wait_split(pe, HT)
                    else:
                        pe.wait_ge(front_read_a, read_a(i, "hid0"))
                    for j in range(2):
                        m = 2 * (name == "hid1") + j
                        last = split_product(front_ps[:, j, :], lambda a, k: w_in[a][:, k, m * P:(m + 1) * P],
                                             lambda b, k: xnT[b][:, q, k, :])
                elif name == "weightsT":
                    pe.wait_ge(rw_ready, i + 1)
                    for c in range(TT):
                        last = pe.transpose(front_ps[0:X, 0, c * P:(c + 1) * P], rw[:, c, :], ident[:, :])
                elif name == "low":
                    pe.wait_ge(front_read_a, read_a(i, "weightsT"))
                    if first_pair(i):
                        pe.wait_ge(w_front_loaded, 2 * 16)
                    pe.wait_ge(u2_ready, i + 1)
                    for e in range(ET):
                        last = pe.matmul(front_ps[:, 0, :], w_x[:, e, 0:R], u2[:, q, e, :], start=(e == 0), stop=(e == ET - 1))
                    for e in range(ET):
                        last = pe.matmul(front_ps[0:2 * NS, 1, :], w_x[:, e, R:R + 2 * NS], u2[:, q, e, :],
                                         start=(e == 0), stop=(e == ET - 1))
                elif name == "C":
                    pe.wait_ge(front_read_a, read_a(i, "dt1"))
                    for c in range(TT):
                        last = pe.matmul(front_ps[:, 0, c * 2 * NS:(c + 1) * 2 * NS], bcT[:, c * P:(c + 1) * P],
                                         ident[0:2 * NS, 0:2 * NS], start=True, stop=True)
                elif name in ("dt0", "dt1"):
                    pe.wait_ge(front_read_a, read_a(i, "low" if name == "dt0" else "dt0"))
                    for j in range(2):
                        m = 2 * (name == "dt1") + j
                        last = pe.matmul(front_ps[:, j, :], w_dt[:, m * P:(m + 1) * P], low[:, :], start=True, stop=True)
                last.then_inc(front_filled, 1)

            def gate(i, q, half, last):
                if half == 0:
                    if not last:
                        pe.wait_ge(front_read_a, read_a(i + 1, "C"))
                    else:
                        pe.wait_ge(gate_read, 2 * i)
                else:
                    pe.wait_ge(gate_read, 2 * i + 1)
                for j in range(2):
                    m = ET + 2 * half + j
                    done = split_product(front_ps[:, j, :], lambda a, k: w_in[a][:, k, m * P:(m + 1) * P],
                                         lambda b, k: xnT[b][:, q, k, :])
                done.then_inc(gate_filled, 1)

            def turn(i, n, m):
                pe.wait_ge(scanned, i * NS + n + 1)
                if n > 0:
                    pe.wait_ge(added, i * NS + n)
                elif not (isinstance(i, int) and i == 0):
                    pe.wait_ge(y_ready, 2 * i - 1)
                for c in range(TT):
                    for e in range(ET):
                        last = pe.transpose(turn_ps[:, c, e * P:(e + 1) * P], state[:, m, e, c * P:(c + 1) * P], ident[:, :])
                last.then_inc(turned, 1)

            def turn_y(i):
                pe.wait_ge(added, (i + 1) * NS)
                for e in range(ET):
                    for c in range(TT):
                        at = (e % 2) * T + c * P
                        last = pe.transpose(turn_ps[:, e // 2, at:at + P], acc[:, c, e * P:(e + 1) * P], ident[:, :])
                last.then_inc(y_turned, 1)

            def pair_in(i, q, p, which):
                if isinstance(i, int) and i == 0:
                    group = (2 * p + 1) * WGROUPS // UT
                    wait_split(pe, HT + (group + 1) * 2 * HT)
                if which == 0 and not (isinstance(i, int) and i == 0 and p < 2):
                    pe.wait_ge(pair_mul, i * PAIRS + p - 1)
                for j in range(2):
                    t = 2 * p + j
                    last = split_product(pair_ps[:, p % 2, which, j, :], lambda a, k: (w_gate, w_up)[which][a][:, k, t * P:(t + 1) * P],
                                         lambda b, k: xnT[b][:, q, k, :])
                if which == 1:
                    last.then_inc(pair_filled, 1)

            def pair_out(i, p):
                pe.wait_ge(w_down_loaded[p % RING], (i * (PAIRS // RING) + p // RING + 1) * 2 * 16)
                pe.wait_ge(pair_ready, i * PAIRS + p + 1)
                if p == 0 and not first_pair(i):
                    pe.wait_ge(res_ready, i)
                for j in range(2):
                    for c in range(TT):
                        last = pe.matmul(out_ps[:, c, :], moe[:, p % RING, j, c * P:(c + 1) * P], w_down[:, p % RING, j, :],
                                         start=(p == 0 and j == 0 and c == 0), stop=False, skip_group_check=True)
                last.then_inc(pair_used, 1)

            def project_y(i, q):
                if isinstance(i, int) and i == 0:
                    pe.wait_ge(w_late_loaded, 16)
                pe.wait_ge(y_ready, 2 * i + 2)
                for e in range(ET):
                    for c in range(TT):
                        last = pe.matmul(out_ps[:, c, :], u2[:, q, e, c * P:(c + 1) * P], w_out[:, e, :],
                                         start=False, stop=(e == ET - 1), skip_group_check=True)
                last.then_inc(out_filled, 1)

            for name in FRONT:
                front(name, 0, 0)
                if name in AHEAD_AFTER:
                    for which in range(2):
                        pair_in(0, 0, AHEAD_AFTER.index(name), which)

            def main(i, q, first, last):
                for s in range(NS):
                    if s == 0 and not first:
                        turn(i - 1, NS - 1, 1)
                    if s > 2:
                        turn(i, s - 1, (s - 1) % 2)
                    for h in halves(s):
                        p, which = h // 2, h % 2
                        if not (first and p < len(AHEAD_AFTER)):
                            pair_in(i, q, p, which)
                        if which == 1 and p >= 2:
                            pair_out(i, p - 2)
                        elif which == 1 and not first:
                            pair_out(i - 1, PAIRS - 2 + p)
                        if s == 1 and h == min(halves(1)) and not first:
                            turn_y(i - 1)
                    if s in (1, 2):
                        turn(i, s - 1, (s - 1) % 2)
                    if s == 2 and not first:
                        project_y(i - 1, 1 - q)
                    for name in FRONT:
                        if not last and STEP[name] == s:
                            front(name, i + 1, 1 - q)
                    if s in GATE_STEP:
                        gate(i, q, GATE_STEP.index(s), last)

            blocks(pe, main)
            end = BLOCKS - 1
            turn(end, NS - 1, 1)
            pair_out(end, PAIRS - 2)
            pair_out(end, PAIRS - 1)
            turn_y(end)
            project_y(end, 1)


_INS = ['L0_attn_input_states', 'L0_attn_W_in', 'L0_attn_conv_kernel', 'L0_attn_conv_bias', 'L0_attn_W_x',
        'L0_attn_W_dt', 'L0_attn_b_dt', 'L0_attn_W_out', 'L0_attn_A_log', 'L0_attn_D', 'L0_ffn_router_w',
        'L0_ffn_w_gate', 'L0_ffn_w_up', 'L0_ffn_w_down']


def kernel(**inputs):
    import numpy as _np
    import concourse.bacc as _bacc
    from concourse import mybir as _mybir
    from concourse.bass_utils import run_bass_kernel_spmd as _run

    nc = _bacc.Bacc("TRN2", target_bir_lowering=False, num_devices=1)
    arrays, args = {}, []
    for name in _INS:
        a = _np.ascontiguousarray(inputs[name])
        arrays[f"in_{name}_dram"] = a
        args.append(nc.dram_tensor(f"in_{name}_dram", a.shape, _mybir.dt.from_np(a.dtype), kind="ExternalInput").ap())
    shape = inputs['L0_attn_input_states'].shape
    args.append(nc.dram_tensor("out_0_dram", shape, _mybir.dt.float32, kind="ExternalOutput").ap())
    build(nc, *args)
    r = _run(nc, [arrays], core_ids=[0])
    return r.results[0]["out_0_dram"]
```
